# Optimizing a Trainium2 kernel written in Bass

```python
import numpy as np
import jax
import jax.numpy as jnp

def _softmax(x, axis=-1):
    return jax.nn.softmax(x, axis=axis)

def _gelu(x):
    return jax.nn.gelu(x, approximate=True)

def _silu(x):
    return jax.nn.silu(x)

def _sigmoid(x):
    return jax.nn.sigmoid(x)

def _layernorm(x, axis=-1, eps=1e-05):
    m = jnp.mean(x, axis=axis, keepdims=True)
    v = jnp.var(x, axis=axis, keepdims=True)
    return (x - m) / jnp.sqrt(v + eps)

def _scatter_add(tgt, idx, src, axis=0):
    return tgt.at[idx].add(src)

def _segment_sum(src, seg, n):
    return jax.ops.segment_sum(src, seg, n)
kernel_name = 'mk_flamingo_gated_d1_seqx_r8_360318'

def setup_inputs(seed: int=0):
    np.random.seed(seed)
    _w = jnp.asarray

    def _rec_inputs():
        import jax
        import jax.numpy as jnp
        _rk = jax.random.key(seed)
        x = 7.22e-05 + 1 * jax.random.normal(jax.random.fold_in(_rk, 1), (8, 128, 512), jnp.float32)
        _lenS = 128 - jax.random.randint(jax.random.fold_in(_rk, 7), (8,), 0, max(1, 128 // 4) + 1, jnp.int32)
        _lenS2 = 128 - jax.random.randint(jax.random.fold_in(_rk, 8), (8,), 0, max(1, 128 // 4) + 1, jnp.int32)
        _ctx_4096P = jax.random.normal(jax.random.fold_in(_rk, 11), (8, 16, 512), jnp.float32)
        _ctx_4096c = jax.random.dirichlet(jax.random.fold_in(_rk, 511), 0.3 * jnp.ones((16,), jnp.float32), (8, 128))
        _ctx_4096t = jnp.einsum('bsk,bkd->bsd', _ctx_4096c, _ctx_4096P)
        _ctx_4096t = _ctx_4096t * jax.lax.rsqrt(jnp.mean(jnp.square(_ctx_4096t)) + 1e-12) * 0.953939
        ctx_4096 = 4.13588e-05 + 0.999923 * (_ctx_4096t + 0.3 * jax.random.normal(jax.random.fold_in(_rk, 611), (8, 128, 512), jnp.float32))
        _validS = jnp.arange(128)[None, :] < _lenS[:, None]
        _validS2 = jnp.arange(128)[None, :] < _lenS2[:, None]
        _causal = jnp.tril(jnp.ones((128, 128), dtype=bool))
        mask_BxSxS2_bk0 = jnp.logical_not(jnp.broadcast_to(_validS2[:, None, :], (8, 128, 128)))
        _g = jax.random.normal(jax.random.fold_in(_rk, 9001), (2, 1), jnp.float32)
        _g = jnp.sign(_g) * jnp.maximum(jnp.abs(_g), 1.0) + (_g == 0) * 1.0
        g_xattn = _g[0]
        g_ffn = _g[1]
        return (x, ctx_4096, mask_BxSxS2_bk0, g_xattn, g_ffn)
    x, ctx_4096, mask_BxSxS2_bk0, g_xattn, g_ffn = _rec_inputs()

    def _L0_xattn_setup():
        import jax, jax.numpy as jnp
        import numpy as np
        B, LQ, LK, D, H, DH = (2, 128, 128, 512, 32, 128)
        EPS = 1e-05

        def _rmsnorm(x, weight):
            var = jnp.mean(jnp.square(x), axis=-1, keepdims=True)
            return x * jax.lax.rsqrt(var + EPS) * weight
        key = jax.random.key(seed)
        ks = jax.random.split(key, 8)
        scale = 0.02
        return {'hidden_states': jax.random.normal(ks[0], (B, LQ, D), jnp.float32), 'key_value_states': jax.random.normal(ks[1], (B, LK, D), jnp.float32), 'attention_mask': jax.random.randint(ks[2], (B, LQ, LK), 0, 2) > 0, 'position_bias': jax.random.normal(ks[3], (H, LQ, LK), jnp.float32), 'ln_weight': jnp.ones((D,), jnp.float32), 'w_q': jax.random.normal(ks[4], (H * DH, D), jnp.float32) * scale, 'w_k': jax.random.normal(ks[5], (H * DH, D), jnp.float32) * scale, 'w_v': jax.random.normal(ks[6], (H * DH, D), jnp.float32) * scale, 'w_out': jax.random.normal(ks[7], (D, H * DH), jnp.float32) * scale}
    _L0_xattn_all = _L0_xattn_setup()
    _L0_xattn_in = {k: v for k, v in _L0_xattn_all.items() if k in ('position_bias', 'ln_weight', 'w_q', 'w_k', 'w_v', 'w_out')}
    del _L0_xattn_all

    def _L0_ffn_setup():
        import jax, jax.numpy as jnp
        import numpy as np
        BATCH, TOK, DIM, OUT = (4, 256, 512, 512)
        E, R, TOP_K = (8, 16, 2)
        SCALING = 16.0 / R
        key = jax.random.key(seed)
        ks = jax.random.split(key, 6)
        return {'x': jax.random.normal(ks[0], (BATCH, TOK, DIM), dtype=jnp.float32), 'W_base': jax.random.normal(ks[1], (OUT, DIM), dtype=jnp.float32) / np.sqrt(DIM), 'b_base': jax.random.normal(ks[2], (OUT,), dtype=jnp.float32) * 0.01, 'W_gate': jax.random.normal(ks[3], (E, DIM), dtype=jnp.float32) * 0.01, 'A': jax.random.normal(ks[4], (E, R, DIM), dtype=jnp.float32) / np.sqrt(DIM), 'B': jax.random.normal(ks[5], (OUT, OUT // OUT * R * 0 + R), dtype=jnp.float32)[None].repeat(E, 0) * 0.0 + jax.random.normal(ks[5], (E, OUT, R), dtype=jnp.float32) * 0.02}
    _L0_ffn_all = _L0_ffn_setup()
    _L0_ffn_in = {k: v for k, v in _L0_ffn_all.items() if k in ('W_base', 'b_base', 'W_gate', 'A', 'B')}
    del _L0_ffn_all
    return {'x': x, 'ctx_4096': ctx_4096, 'mask_BxSxS2_bk0': mask_BxSxS2_bk0, 'g_xattn': g_xattn, 'g_ffn': g_ffn, 'L0_xattn_position_bias': _L0_xattn_in['position_bias'], 'L0_xattn_ln_weight': _L0_xattn_in['ln_weight'], 'L0_xattn_w_q': _L0_xattn_in['w_q'], 'L0_xattn_w_k': _L0_xattn_in['w_k'], 'L0_xattn_w_v': _L0_xattn_in['w_v'], 'L0_xattn_w_out': _L0_xattn_in['w_out'], 'L0_ffn_W_base': _L0_ffn_in['W_base'], 'L0_ffn_b_base': _L0_ffn_in['b_base'], 'L0_ffn_W_gate': _L0_ffn_in['W_gate'], 'L0_ffn_A': _L0_ffn_in['A'], 'L0_ffn_B': _L0_ffn_in['B']}

def reference(x, ctx_4096, mask_BxSxS2_bk0, g_xattn, g_ffn, L0_xattn_position_bias, L0_xattn_ln_weight, L0_xattn_w_q, L0_xattn_w_k, L0_xattn_w_v, L0_xattn_w_out, L0_ffn_W_base, L0_ffn_b_base, L0_ffn_W_gate, L0_ffn_A, L0_ffn_B):
    import jax
    import jax.numpy as jnp

    def _L0_xattn_ref(hidden_states, key_value_states, attention_mask, position_bias, ln_weight, w_q, w_k, w_v, w_out):
        import jax, jax.numpy as jnp
        import numpy as np
        B, LQ, LK, D, H, DH = (2, 128, 128, 512, 32, 128)
        EPS = 1e-05

        def _rmsnorm(x, weight):
            var = jnp.mean(jnp.square(x), axis=-1, keepdims=True)
            return x * jax.lax.rsqrt(var + EPS) * weight
        x = _rmsnorm(hidden_states, ln_weight)
        b, lq, _ = x.shape
        lk = key_value_states.shape[1]
        h_q = (x @ w_q.T).reshape(b, lq, H, DH)
        h_k = (key_value_states @ w_k.T).reshape(b, lk, H, DH)
        h_v = (key_value_states @ w_v.T).reshape(b, lk, H, DH)
        score = jnp.einsum('bqhd,bkhd->bhqk', h_q, h_k)
        score = score + position_bias[None]
        m = attention_mask[:, None]
        score = jnp.where(m, score, -jnp.inf)
        score = jax.nn.softmax(score, axis=-1)
        score = jnp.where(m, score, 0.0)
        attn = jnp.einsum('bhqk,bkhd->bqhd', score, h_v).reshape(b, lq, H * DH)
        out = attn @ w_out.T
        return hidden_states + out

    def _L0_ffn_ref(x, W_base, b_base, W_gate, A, B):
        import jax, jax.numpy as jnp
        import numpy as np
        BATCH, TOK, DIM, OUT = (4, 256, 512, 512)
        E, R, TOP_K = (8, 16, 2)
        SCALING = 16.0 / R
        result = jnp.einsum('bnd,od->bno', x, W_base) + b_base
        logits = jnp.einsum('bnd,ed->bne', x, W_gate)
        probs = jax.nn.softmax(logits.astype(jnp.float32), axis=-1)
        top_p, top_i = jax.lax.top_k(probs, TOP_K)
        top_p = top_p / jnp.sum(top_p, axis=-1, keepdims=True)
        top_p = top_p.astype(x.dtype)
        route_w = jnp.sum(jax.nn.one_hot(top_i, E, dtype=x.dtype) * top_p[..., None], axis=-2)
        h = jnp.einsum('bnd,erd->bner', x, A)
        hw = h * route_w[..., None]
        delta = jnp.einsum('bner,eor->bno', hw, B)
        return result + delta * SCALING
    x = x + jnp.tanh(g_xattn[0]) * _L0_xattn_ref(_layernorm(x, axis=-1), ctx_4096, mask_BxSxS2_bk0, L0_xattn_position_bias, L0_xattn_ln_weight, L0_xattn_w_q, L0_xattn_w_k, L0_xattn_w_v, L0_xattn_w_out)
    x = x + jnp.tanh(g_ffn[0]) * _L0_ffn_ref(_layernorm(x, axis=-1), L0_ffn_W_base, L0_ffn_b_base, L0_ffn_W_gate, L0_ffn_A, L0_ffn_B)
    return x

_drawn_inputs = setup_inputs


def setup_inputs(seed=0):
    import zlib

    import numpy as np

    out = dict(_drawn_inputs(seed))
    spreads = {'L0_xattn_ln_weight': (1.0, 0.558)}
    factors = {'L0_ffn_b_base': 8.0}
    for name, (base, spread) in spreads.items():
        noise = np.random.default_rng([zlib.crc32(name.encode()), seed]).standard_normal(out[name].shape)
        drawn = base * np.exp(spread * noise) if base else spread * noise
        out[name] = jnp.asarray(drawn.astype(out[name].dtype))
    for name, factor in factors.items():
        out[name] = (out[name] * factor).astype(out[name].dtype)
    return out
```

```python
from contextlib import ExitStack

import concourse.bass as bass
from concourse import mybir

ALU = mybir.AluOpType
ACT = mybir.ActivationFunctionType
F32 = mybir.dt.float32
F32R = mybir.dt.float32r
U8 = mybir.dt.uint8
U32 = mybir.dt.uint32
AX_X = mybir.AxisListType.X

P = 128
B = 8
D = 512
C = D // P
H = 32
GH = 4
G = H // GH
T = B * P
HALF = B // 2
E = 8
R = 16
ER = E * R
AG = ER + E
EPS = 1e-5
MASKED = -1e30
LAST = H - 1
BANK = 512



def split_before(h):
    if isinstance(h, int) and h < 0:
        return 8
    if isinstance(h, int) and h > 28:
        return {29: 126, 30: 129, 31: 132, 32: 134}[h]
    return 4 * h + 10


def split_q(h):
    if isinstance(h, int) and h < 3:
        return 5 + 2 * h
    return 4 * h + 1


def stage_count(n):
    if isinstance(n, int) and n > 28:
        return {29: 1040, 30: 1072, 31: 1072}[n]
    return 32 * n + 128


def bias_count(h, parity):
    return 8 * h + (16 if parity == 0 else 8)


def program(nc, x, ctx, mask, gates, bias, ln_w, w_q, w_k, w_v, w_o, w_base, b_base, w_ag, w_b, out):
    with ExitStack() as stack:
        def sb(name, shape, dt=F32):
            return stack.enter_context(nc.sbuf_tensor(name, shape, dt))

        def pb(name):
            return stack.enter_context(nc.psum_tensor(name, [P, BANK], F32))

        def sem(name):
            return stack.enter_context(nc.semaphore(name))

        xT_hi, xT_lo = sb("xT_hi", [P, C, T], F32R), sb("xT_lo", [P, C, T], F32R)
        ctxT_hi, ctxT_lo = sb("ctxT_hi", [P, C, T], F32R), sb("ctxT_lo", [P, C, T], F32R)
        acc = sb("acc", [P, B, D])
        wq_hi, wq_lo = sb("wq_hi", [P, 2, C, P], F32R), sb("wq_lo", [P, 2, C, P], F32R)
        wk_hi, wk_lo = sb("wk_hi", [P, 2, C, P], F32R), sb("wk_lo", [P, 2, C, P], F32R)
        wv_hi, wv_lo = sb("wv_hi", [P, C, GH * P], F32R), sb("wv_lo", [P, C, GH * P], F32R)
        wo_hi, wo_lo = sb("wo_hi", [P, 2, D], F32R), sb("wo_lo", [P, 2, D], F32R)
        ag_hi, ag_lo = sb("ag_hi", [P, C, AG], F32R), sb("ag_lo", [P, C, AG], F32R)
        stage = sb("stage", [P, 2, 4, D])
        qT, kT = sb("qT", [P, T]), sb("kT", [P, T])
        v = sb("v", [P, B, GH * P])
        probs, probsT = sb("probs", [P, B, P]), sb("probsT", [P, B, P])
        attn_hi, attn_lo = sb("attn_hi", [P, 2, T], F32R), sb("attn_lo", [P, 2, T], F32R)
        pos_bias = sb("pos_bias", [P, 2, P])
        mask8 = sb("mask8", [P, B, P], U8)
        mask_bias, full_bias = sb("mask_bias", [P, B, P]), sb("full_bias", [P, B, P])
        row_any = sb("row_any", [P, B])
        neg_max, sums, sums_inv, prob_scale = (sb(n, [P, B]) for n in ("neg_max", "sums", "sums_inv", "prob_scale"))
        ident = sb("ident", [P, P])
        ln_w_sb = sb("ln_w_sb", [P, C])
        gates_sb, gates_tanh = sb("gates_sb", [P, 2]), sb("gates_tanh", [P, 2])
        b_base_sb = sb("b_base_sb", [P, D])
        half_neg = sb("half_neg", [P, B])
        experts = sb("experts", [P, E])
        stats, moments = sb("stats", [P, B, 6]), sb("moments", [P, B, 2])
        var_eps, rstd, rms_in, rms_inv, x_scale = (
            sb(n, [P, B]) for n in ("var_eps", "rstd", "rms_in", "rms_inv", "x_scale"))
        logits, top8, top_i = sb("logits", [P, 2, E]), sb("top8", [P, 2, 8]), sb("top_i", [P, 2, 8], U32)
        top_f = sb("top_f", [P, 2, 2])
        gap, ratio, ratio1, w_first, w_second = (
            sb(n, [P, 2]) for n in ("gap", "ratio", "ratio1", "w_first", "w_second"))
        route1, route2, route = (sb(n, [P, 2, E]) for n in ("route1", "route2", "route"))
        hw = sb("hw", [P, 2, ER])
        hwT_hi, hwT_lo = sb("hwT_hi", [P, 2, P], F32R), sb("hwT_lo", [P, 2, P], F32R)

        wb_hi = wq_hi[:, 0, :, :].rearrange("p c n -> p (c n)")
        wb_lo = wq_lo[:, 0, :, :].rearrange("p c n -> p (c n)")
        ag_raw = stage[:, 1, 2:4, :].rearrange("p a n -> p (a n)")[:, 0:C * AG]
        x_norm = [probs[:, 0:4, :], probs[:, 4:8, :], probsT[:, 0:4, :], probsT[:, 4:8, :]]
        ctx_raw = [v[:, b, :].rearrange("p (c t) -> p c t", c=C) for b in range(B)]

        proj = [pb("proj0"), pb("proj1")]
        score = [pb("score0"), pb("score1")]
        turned = [pb("turned0"), pb("turned1")]
        attended = [pb("attended0"), pb("attended1")]

        stage_loaded = [sem("stage_loaded0"), sem("stage_loaded1")]
        bias_loaded = [sem("bias_loaded0"), sem("bias_loaded1")]
        ctx_loaded = [sem(f"ctx_loaded{i}") for i in range(4)]
        x_loaded = [sem("x_loaded0"), sem("x_loaded1")]
        small_loaded = sem("small_loaded")
        out_stored = sem("out_stored")
        hi_made, lo_made = sem("hi_made"), sem("lo_made")
        ident_made, consts_made, mask_made, mask_chain = (
            sem(n) for n in ("ident_made", "consts_made", "mask_made", "mask_chain"))
        ctx_hi_made, ctx_lo_made = sem("ctx_hi_made"), sem("ctx_lo_made")
        ln_chain, ln_pow = sem("ln_chain"), sem("ln_pow")
        x_normed, x_turned, x_hi_made, x_lo_made = (
            sem(n) for n in ("x_normed", "x_turned", "x_hi_made", "x_lo_made"))
        h_made, tanh_made = sem("h_made"), sem("tanh_made")
        qk_projected, qk_copied = sem("qk_projected"), sem("qk_copied")
        v_projected, v_copied = sem("v_projected"), sem("v_copied")
        bias_made = sem("bias_made")
        scores_made, scores_biased, max_made = sem("scores_made"), sem("scores_biased"), sem("max_made")
        exp_made, sums_inverted, scale_made = sem("exp_made"), sem("sums_inverted"), sem("scale_made")
        probs_scaled, probs_turned, probsT_copied = (
            sem(n) for n in ("probs_scaled", "probs_turned", "probsT_copied"))
        attn_made, attn_hi_made, attn_lo_made = sem("attn_made"), sem("attn_hi_made"), sem("attn_lo_made")
        out_projected, out_added = sem("out_projected"), sem("out_added")
        x1_made, f_chain, f_var, f_pow = sem("x1_made"), sem("f_chain"), sem("f_var"), sem("f_pow")
        y_made, y_turned, y_hi_made, y_lo_made = (
            sem(n) for n in ("y_made", "y_turned", "y_hi_made", "y_lo_made"))
        ag_projected, base_projected = sem("ag_projected"), sem("base_projected")
        gap_made, ratio_made, hw_made, hw_turned = (
            sem(n) for n in ("gap_made", "ratio_made", "hw_made", "hw_turned"))
        hw_hi_made, hw_lo_made, delta_added = sem("hw_hi_made"), sem("hw_lo_made"), sem("delta_added")
        out_made = sem("out_made")

        def run_steps(eng, step):
            for h in range(GH):
                step(h, h % GH)
            with eng.Fori(1, G - 1) as g:
                for j in range(GH):
                    step(g * GH + j, j)
            for h in range(H - GH, H):
                step(h, h % GH)

        def is_last(h):
            return isinstance(h, int) and h == LAST

        def is_first(h):
            return isinstance(h, int) and h == 0

        def pieces(h, j):
            raw = [stage[:, j % 2, i, :] for i in range(4)]
            four = [r.rearrange("p (c n) -> p c n", c=C) for r in raw]
            p = j % 2
            found = []
            if not (isinstance(h, int) and h < 0):
                found += [(wo_hi[:, p, :], wo_lo[:, p, :], raw[0]),
                          (wv_hi[:, j, :], wv_lo[:, j, :], raw[1])]
            if not isinstance(h, int) or h + 3 <= LAST:
                q = (j + 3) % 2
                found += [(wq_hi[:, q, :, :], wq_lo[:, q, :, :], four[2]),
                          (wk_hi[:, q, :, :], wk_lo[:, q, :, :], four[3])]
            elif h == 29:
                found.append((ag_hi[:, :, :], ag_lo[:, :, :], ag_raw.rearrange("p (c n) -> p c n", c=C)))
            elif h == 30:
                found.append((wb_hi, wb_lo, raw[2]))
            return found

        first_v = [(wv_hi[:, c, :], wv_lo[:, c, :], stage[:, 1, c, :]) for c in range(C)]
        first_qk = []
        for i in range(2):
            for k, (hi, lo) in enumerate(((wq_hi, wq_lo), (wk_hi, wk_lo))):
                raw = stage[:, 0, 2 * i + k, :].rearrange("p (c n) -> p c n", c=C)
                first_qk.append((hi[:, i, :, :], lo[:, i, :, :], raw))

        block = stack.enter_context(nc.Block())

        @block.sync
        def _(sp):
            for c in range(C):
                sp.dma_start(stage[:, 1, c, :], w_v[c, :, :]).then_inc(stage_loaded[1], 16)
            for i in range(4):
                sp.dma_start(v[:, 2 * i:2 * i + 2, :], ctx[:, 2 * i:2 * i + 2, :]).then_inc(ctx_loaded[i], 16)
            for i in range(2):
                sp.dma_start(acc[:, HALF * i:HALF * (i + 1), :],
                             x[HALF * i:HALF * (i + 1), :, :].rearrange("b p d -> p b d")).then_inc(x_loaded[i], 16)
            for i in range(2):
                sp.dma_start(stage[:, 0, 2 * i, :], w_q[i, :, :]).then_inc(stage_loaded[0], 16)
                sp.dma_start(stage[:, 0, 2 * i + 1, :], w_k[i, :, :]).then_inc(stage_loaded[0], 16)
            sp.dma_start(mask8[:, :, :], mask).then_inc(small_loaded, 16)
            sp.dma_start(ln_w_sb[:, :], ln_w).then_inc(small_loaded, 16)
            sp.dma_start(gates_sb[:, :], gates.partition_broadcast(P)).then_inc(small_loaded, 16)
            sp.dma_start(b_base_sb[:, :], b_base.partition_broadcast(P)).then_inc(small_loaded, 16)
            for i in range(2):
                sp.dma_start(pos_bias[:, i, :], bias[i, :, :]).then_inc(bias_loaded[i], 16)
            sp.wait_ge(lo_made, 4)
            sp.dma_start(stage[:, 1, 2, :], w_q[2, :, :]).then_inc(stage_loaded[1], 16)
            sp.dma_start(stage[:, 1, 3, :], w_k[2, :, :]).then_inc(stage_loaded[1], 16)

            def step(n, j):
                p = j % 2
                sp.wait_ge(lo_made, split_before(n - 1))
                sp.dma_start(stage[:, p, 0, :], w_o[n, :, :]).then_inc(stage_loaded[p], 16)
                wide = w_base[j, :, :] if isinstance(n, int) and n >= H - GH else w_v[n + GH, :, :]
                sp.dma_start(stage[:, p, 1, :], wide).then_inc(stage_loaded[p], 16)
                if not isinstance(n, int) or n + 3 <= LAST:
                    sp.dma_start(stage[:, p, 2, :], w_q[n + 3, :, :]).then_inc(stage_loaded[p], 16)
                    sp.dma_start(stage[:, p, 3, :], w_k[n + 3, :, :]).then_inc(stage_loaded[p], 16)
                elif n == 29:
                    sp.dma_start(ag_raw, w_ag).then_inc(stage_loaded[p], 16)
                elif n == 30:
                    sp.dma_start(stage[:, p, 2, :], w_b).then_inc(stage_loaded[p], 16)
                if not isinstance(n, int) or n + 2 <= LAST:
                    sp.wait_ge(bias_made, n + 1)
                    sp.dma_start(pos_bias[:, p, :], bias[n + 2, :, :]).then_inc(bias_loaded[p], 16)

            run_steps(sp, step)

            for i, n in ((0, 31), (1, 32)):
                sp.wait_ge(lo_made, split_before(n))
                sp.dma_start(stage[:, i, :, :],
                             x[HALF * i:HALF * (i + 1), :, :].rearrange("b p d -> p b d")
                             ).then_inc(stage_loaded[i], 16)
            for t in range(B):
                sp.wait_ge(out_made, t + 1)
                sp.dma_start(out[t, :, :], acc[:, t, :]).then_inc(out_stored, 16)
            sp.wait_ge(out_stored, 16 * B)

        @block.gpsimd
        def _(pool):
            pool.memset(ident[:, :], 0.0).then_inc(ident_made, 1)
            pool.memset(half_neg[:, :], -0.5).then_inc(consts_made, 1)
            for e in range(E):
                pool.memset(experts[:, e:e + 1], float(e)).then_inc(consts_made, 1)
            pool.wait_ge(ident_made, 1)
            pool.affine_select(out=ident[:, :], in_=ident[:, :], compare_op=ALU.not_equal, fill=1.0,
                               base=0, pattern=[[-1, P]], channel_multiplier=1).then_inc(ident_made, 1)
            pool.wait_ge(consts_made, 1 + E)

            def make_lo(piece, n):
                hi, lo, raw = piece
                pool.wait_ge(hi_made, n)
                pool.tensor_tensor(lo, raw, hi.bitcast(F32), ALU.subtract).then_inc(lo_made, 1)

            for i, piece in enumerate(first_v):
                make_lo(piece, 1 + i)
            for half in range(2):
                a, b = HALF * half, HALF * (half + 1)
                pool.wait_ge(ln_chain, 4 * half + 1)
                pool.tensor_tensor(rstd[:, a:b], var_eps[:, a:b], half_neg[:, a:b], ALU.pow).then_inc(ln_pow, 1)
                pool.wait_ge(ln_chain, 4 * half + 4)
                pool.tensor_tensor(rms_inv[:, a:b], rms_in[:, a:b], half_neg[:, a:b], ALU.pow).then_inc(ln_pow, 1)
            for i, piece in enumerate(first_qk):
                make_lo(piece, 5 + i)

            def add_bias(h, j):
                p = j % 2
                pool.wait_ge(bias_loaded[p], bias_count(h, p))
                if is_first(h):
                    pool.wait_ge(mask_made, 2)
                else:
                    pool.wait_ge(scores_biased, 2 * h)
                pool.tensor_tensor(full_bias[:, :, :], mask_bias[:, :, :],
                                   pos_bias[:, p, :].unsqueeze(1).broadcast_to([P, B, P]),
                                   ALU.add).then_inc(bias_made, 1)

            add_bias(0, 0)

            def step(h, j):
                found = pieces(h, j)
                n = split_before(h)
                early = 0 if isinstance(h, int) and h < 0 else 2
                for i in range(early):
                    make_lo(found[i], n + 1 + i)
                if not is_last(h):
                    for half in range(2):
                        a, b = HALF * half, HALF * (half + 1)
                        pool.wait_ge(scale_made, 2 * (h + 1) + half + 1)
                        pool.tensor_tensor(probs[:, a:b, :], probs[:, a:b, :],
                                           prob_scale[:, a:b].unsqueeze(2).broadcast_to([P, HALF, P]),
                                           ALU.mult).then_inc(probs_scaled, 1)
                if not isinstance(h, int) or h + 2 <= LAST:
                    add_bias(h + 2, j)
                for i in range(early, len(found)):
                    make_lo(found[i], n + 1 + i)

            step(-1, 3)
            run_steps(pool, step)

            for t in range(B):
                pool.wait_ge(f_var, t + 1)
                pool.tensor_tensor(rstd[:, t:t + 1], var_eps[:, t:t + 1], half_neg[:, t:t + 1],
                                   ALU.pow).then_inc(f_pow, 1)

        @block.scalar
        def _(act):
            def make_hi(piece):
                hi, _, raw = piece
                act.activation(hi, raw, ACT.Copy).then_inc(hi_made, 1)

            def copy_v(g, t):
                act.wait_ge(v_projected, B * g + t + 1)
                if not (isinstance(g, int) and g == 0):
                    act.wait_ge(attn_made, 2 * (GH * g - 1) + t // HALF + 1)
                act.activation(v[:, t, :], proj[t % 2][:, :], ACT.Copy).then_inc(v_copied, 1)

            act.wait_ge(stage_loaded[1], 16 * C)
            for piece in first_v:
                make_hi(piece)
            for b in range(B):
                act.wait_ge(ctx_loaded[b // 2], 16)
                act.activation(ctxT_hi[:, :, b * P:(b + 1) * P], ctx_raw[b], ACT.Copy).then_inc(ctx_hi_made, 1)
            act.wait_ge(stage_loaded[0], 16 * C)
            for piece in first_qk:
                make_hi(piece)
            act.wait_ge(small_loaded, 16 * 4)
            act.activation(gates_tanh[:, :], gates_sb[:, :], ACT.Tanh).then_inc(tanh_made, 1)
            for t in range(HALF):
                copy_v(0, t)
            for t in range(HALF, B):
                copy_v(0, t)
                for b in (2 * (t - HALF), 2 * (t - HALF) + 1):
                    act.wait_ge(x_turned, b + 1)
                    for c in range(C):
                        ins = act.activation(xT_hi[:, c, b * P:(b + 1) * P], turned[b % 2][:, c * P:(c + 1) * P],
                                             ACT.Identity, scale=ln_w_sb[:, c:c + 1])
                    ins.then_inc(x_hi_made, 1)

            def copy_qk(h):
                for k, dst in enumerate((qT, kT)):
                    for half in range(2):
                        act.wait_ge(qk_projected, 4 * h + 2 * k + half + 1)
                        if not is_first(h):
                            act.wait_ge(scores_made, 2 * (h - 1) + half + 1)
                        act.activation(dst[:, half * BANK:(half + 1) * BANK], proj[half][:, :],
                                       ACT.Copy).then_inc(qk_copied, 1)

            def step(h, j):
                found = pieces(h, j)
                before = isinstance(h, int) and h < 0
                act.wait_ge(stage_loaded[j % 2], stage_count(h))
                if not before:
                    if j % 2 == 0 and not is_first(h):
                        act.wait_ge(out_projected, 4 * h)
                    make_hi(found[0])
                    if j == 0:
                        act.wait_ge(v_projected, 2 * h + B)
                    make_hi(found[1])
                if not is_last(h):
                    copy_qk(h + 1)
                if not before:
                    for half in range(2):
                        act.wait_ge(probs_turned, 2 * h + half + 1)
                        if not is_first(h):
                            act.wait_ge(attn_made, 2 * (h - 1) + half + 1)
                        act.activation(probsT[:, HALF * half:HALF * (half + 1), :], turned[half][:, :],
                                       ACT.Copy).then_inc(probsT_copied, 1)
                    for half in range(2):
                        act.wait_ge(attn_made, 2 * h + half + 1)
                        if j % 2 == 0 and half == 0 and not is_first(h):
                            act.wait_ge(out_projected, 4 * h)
                        act.activation(attn_hi[:, j % 2, half * BANK:(half + 1) * BANK], attended[half][:, :],
                                       ACT.Copy).then_inc(attn_hi_made, 1)
                if not is_last(h):
                    for half in range(2):
                        act.wait_ge(max_made, 2 * (h + 1) + half + 1)
                        for b in range(HALF * half, HALF * (half + 1)):
                            ins = act.activation(probs[:, b, :], probs[:, b, :], ACT.Exp, bias=neg_max[:, b:b + 1],
                                                 scale=1.0, accum_out=sums[:, b:b + 1])
                        ins.then_inc(exp_made, 1)
                for piece in found[0 if before else 2:]:
                    make_hi(piece)
                if j == GH - 1 and not before and not is_last(h):
                    for t in range(B):
                        copy_v_next(h, t)

            def copy_v_next(h, t):
                act.wait_ge(v_projected, 2 * (h + 1) + t + 1)
                act.wait_ge(attn_made, 2 * h + t // HALF + 1)
                act.activation(v[:, t, :], proj[t % 2][:, :], ACT.Copy).then_inc(v_copied, 1)

            step(-1, 3)
            run_steps(act, step)

            for t in range(B + 1):
                if t < B:
                    act.wait_ge(y_turned, t + 1)
                    if t >= 2:
                        act.wait_ge(base_projected, t - 1)
                    act.activation(xT_hi[:, :, (t % 2) * P:(t % 2 + 1) * P],
                                   score[t % 2][:, :].rearrange("p (c t) -> p c t", c=C),
                                   ACT.Copy).then_inc(y_hi_made, 1)
                if t >= 1:
                    u = t - 1
                    act.wait_ge(gap_made, u + 1)
                    act.activation(ratio[:, u % 2:u % 2 + 1], gap[:, u % 2:u % 2 + 1], ACT.Exp).then_inc(ratio_made, 1)
                    act.wait_ge(hw_turned, u + 1)
                    if u >= 2:
                        act.wait_ge(delta_added, u - 1)
                    act.activation(hwT_hi[:, u % 2, :], attended[u % 2][:, 0:P], ACT.Copy).then_inc(hw_hi_made, 1)

        @block.vector
        def _(dve):
            dve.wait_ge(small_loaded, 16 * 4)
            dve.tensor_scalar(mask_bias[:, :, :], mask8[:, :, :], -MASKED, MASKED, ALU.mult, ALU.add).then_inc(mask_made, 1)
            dve.tensor_reduce(row_any[:, :], mask8[:, :, :], AX_X, ALU.max).then_inc(mask_made, 1)
            for b in range(B):
                dve.wait_ge(ctx_hi_made, b + 1)
                at = slice(b * P, (b + 1) * P)
                dve.tensor_tensor(ctxT_lo[:, :, at], ctx_raw[b], ctxT_hi[:, :, at].bitcast(F32),
                                  ALU.subtract).then_inc(ctx_lo_made, 1)

            def norm_x(half):
                a, b = HALF * half, HALF * (half + 1)
                dve.wait_ge(x_loaded[half], 16)
                for t in range(a, b):
                    dve.bn_stats(stats[:, t, :], acc[:, t, :]).then_inc(f_chain, 1)
                dve.wait_ge(f_chain, 2 * b - HALF)
                for t in range(a, b):
                    dve.bn_aggr(moments[:, t, :], stats[:, t, :]).then_inc(f_chain, 1)
                dve.wait_ge(f_chain, 2 * b)
                mean, var = moments[:, a:b, 0], moments[:, a:b, 1]
                dve.tensor_scalar(var_eps[:, a:b], var, EPS, None, ALU.add).then_inc(ln_chain, 1)
                dve.wait_ge(ln_pow, 2 * half + 1)
                dve.tensor_tensor(rms_in[:, a:b], var, rstd[:, a:b], ALU.mult).then_inc(ln_chain, 1)
                dve.wait_ge(ln_chain, 4 * half + 2)
                dve.tensor_tensor(rms_in[:, a:b], rms_in[:, a:b], rstd[:, a:b], ALU.mult).then_inc(ln_chain, 1)
                dve.wait_ge(ln_chain, 4 * half + 3)
                dve.tensor_scalar(rms_in[:, a:b], rms_in[:, a:b], EPS, None, ALU.add).then_inc(ln_chain, 1)
                dve.wait_ge(ln_pow, 2 * half + 2)
                dve.tensor_tensor(x_scale[:, a:b], rstd[:, a:b], rms_inv[:, a:b], ALU.mult).then_inc(mask_chain, 1)
                dve.wait_ge(mask_chain, half + 1)
                for t in range(a, b):
                    if half:
                        dve.wait_ge(x_turned, t - HALF + 1)
                    dve.tensor_scalar(x_norm[t % HALF], acc[:, t, :].rearrange("p (c n) -> p c n", c=C),
                                      moments[:, t, 0:1], x_scale[:, t:t + 1],
                                      ALU.subtract, ALU.mult).then_inc(x_normed, 1)
                dve.wait_ge(x_normed, b)
                for t in range(a, b):
                    dve.tensor_scalar(acc[:, t, :], acc[:, t, :], moments[:, t, 0:1], rstd[:, t:t + 1],
                                      ALU.subtract, ALU.mult).then_inc(h_made, 1)

            def x_lo(t):
                dve.wait_ge(x_hi_made, t + 1)
                for c in range(C):
                    at = slice(t * P, (t + 1) * P)
                    ins = dve.scalar_tensor_tensor(out=xT_lo[:, c, at], in0=turned[t % 2][:, c * P:(c + 1) * P],
                                                   scalar=ln_w_sb[:, c:c + 1], in1=xT_hi[:, c, at].bitcast(F32),
                                                   op0=ALU.mult, op1=ALU.subtract)
                ins.then_inc(x_lo_made, 1)

            norm_x(0)
            for t in range(2):
                x_lo(t)
            x_lo(2)
            x_lo(3)
            norm_x(1)
            for t in range(HALF, B):
                x_lo(t)

            def bias_and_max(h, j):
                for half in range(2):
                    a, b = HALF * half, HALF * (half + 1)
                    dve.wait_ge(scores_made, 2 * h + half + 1)
                    dve.wait_ge(bias_made, h + 1)
                    if not is_first(h):
                        dve.wait_ge(probs_turned, 2 * (h - 1) + half + 1)
                    dve.tensor_tensor(probs[:, a:b, :], score[half][:, :].rearrange("p (b k) -> p b k", b=HALF),
                                      full_bias[:, a:b, :], ALU.add).then_inc(scores_biased, 1)
                    dve.wait_ge(scores_biased, 2 * h + half + 1)
                    dve.tensor_reduce(neg_max[:, a:b], probs[:, a:b, :], AX_X, ALU.max,
                                      negate=True).then_inc(max_made, 1)

            def prob_scales(h, half):
                a, b = HALF * half, HALF * (half + 1)
                dve.wait_ge(exp_made, 2 * h + half + 1)
                dve.reciprocal(sums_inv[:, a:b], sums[:, a:b]).then_inc(sums_inverted, 1)
                dve.wait_ge(sums_inverted, 2 * h + half + 1)
                dve.tensor_tensor(prob_scale[:, a:b], sums_inv[:, a:b], row_any[:, a:b], ALU.mult).then_inc(scale_made, 1)

            def add_out(h, t):
                dve.wait_ge(out_projected, 4 * (h - 1) + t + 1)
                dve.tensor_tensor(acc[:, t, :], proj[t % 2][:, :], acc[:, t, :], ALU.add).then_inc(out_added, 1)

            def step(h, j):
                before = isinstance(h, int) and h < 0
                if not is_last(h):
                    bias_and_max(h + 1, j)
                if not before:
                    for half in range(2):
                        dve.wait_ge(attn_hi_made, 2 * h + half + 1)
                        at = slice(half * BANK, (half + 1) * BANK)
                        dve.tensor_tensor(attn_lo[:, j % 2, at], attended[half][:, :],
                                          attn_hi[:, j % 2, at].bitcast(F32), ALU.subtract).then_inc(attn_lo_made, 1)
                if j % 2 == 1 and not before:
                    if not (isinstance(h, int) and h == 1):
                        dve.wait_ge(out_added, 4 * (h - 1))
                    if j == GH - 1 and not is_last(h):
                        prob_scales(h + 1, 0)
                        prob_scales(h + 1, 1)
                        for t in range(B):
                            add_out(h, t)
                    else:
                        for t in range(B):
                            add_out(h, t)
                            if t in (1, 3) and not is_last(h):
                                prob_scales(h + 1, t // 2)
                            if is_last(h):
                                norm_y_begin(t)
                elif not is_last(h):
                    prob_scales(h + 1, 0)
                    prob_scales(h + 1, 1)

            def norm_y_begin(t):
                x1 = stage[:, t // HALF, t % HALF, :]
                dve.wait_ge(stage_loaded[t // HALF], 1088)
                dve.wait_ge(out_added, 4 * (LAST - 1) + t + 1)
                dve.scalar_tensor_tensor(out=x1, in0=acc[:, t, :], scalar=gates_tanh[:, 0:1], in1=x1,
                                         op0=ALU.mult, op1=ALU.add).then_inc(x1_made, 1)
                n = 2 * B + 2 * t
                dve.wait_ge(x1_made, t + 1)
                dve.bn_stats(stats[:, t, :], x1).then_inc(f_chain, 1)
                dve.wait_ge(f_chain, n + 1)
                dve.bn_aggr(moments[:, t, :], stats[:, t, :]).then_inc(f_chain, 1)
                dve.wait_ge(f_chain, n + 2)
                dve.tensor_scalar(var_eps[:, t:t + 1], moments[:, t, 1:2], EPS, None, ALU.add).then_inc(f_var, 1)

            dve.wait_ge(tanh_made, 1)
            step(-1, 3)
            run_steps(dve, step)

            def norm_y(t):
                dve.wait_ge(f_pow, t + 1)
                x1 = stage[:, t // HALF, t % HALF, :]
                dve.tensor_scalar(acc[:, t, :], x1, moments[:, t, 0:1], rstd[:, t:t + 1],
                                  ALU.subtract, ALU.mult).then_inc(y_made, 1)

            def y_lo(t):
                dve.wait_ge(y_hi_made, t + 1)
                at = slice((t % 2) * P, (t % 2 + 1) * P)
                dve.tensor_tensor(xT_lo[:, :, at], score[t % 2][:, :].rearrange("p (c t) -> p c t", c=C),
                                  xT_hi[:, :, at].bitcast(F32), ALU.subtract).then_inc(y_lo_made, 1)

            route_steps = [0]

            def after(ins):
                route_steps[0] += 1
                ins.then_inc(ln_chain, 1)
                dve.wait_ge(ln_chain, 2 * 4 + route_steps[0])

            def route_tile(t):
                p = t % 2
                one = slice(p, p + 1)
                dve.wait_ge(ag_projected, t + 1)
                after(dve.tensor_copy(logits[:, p, :], turned[p][:, ER:AG]))
                after(dve.max(top8[:, p, :], logits[:, p, :]))
                dve.tensor_tensor(gap[:, one], top8[:, p, 1:2], top8[:, p, 0:1], ALU.subtract).then_inc(gap_made, 1)
                after(dve.max_index(top_i[:, p, :], top8[:, p, :], logits[:, p, :]))
                after(dve.tensor_copy(top_f[:, p, :], top_i[:, p, 0:2]))
                dve.wait_ge(ratio_made, t + 1)
                after(dve.tensor_scalar(ratio1[:, one], ratio[:, one], 1.0, None, ALU.add))
                after(dve.reciprocal(w_first[:, one], ratio1[:, one]))
                after(dve.tensor_tensor(w_second[:, one], ratio[:, one], w_first[:, one], ALU.mult))
                dve.tensor_scalar(route1[:, p, :], experts[:, :], top_f[:, p, 0:1], w_first[:, one],
                                  ALU.is_equal, ALU.mult)
                after(dve.tensor_scalar(route2[:, p, :], experts[:, :], top_f[:, p, 1:2], w_second[:, one],
                                        ALU.is_equal, ALU.mult))
                after(dve.tensor_tensor(route[:, p, :], route1[:, p, :], route2[:, p, :], ALU.add))
                dve.tensor_tensor(hw[:, p, :].rearrange("p (e r) -> p e r", e=E),
                                  turned[p][:, 0:ER].rearrange("p (e r) -> p e r", e=E),
                                  route[:, p, :].unsqueeze(2).broadcast_to([P, E, R]), ALU.mult).then_inc(hw_made, 1)

            def hw_lo(t):
                dve.wait_ge(hw_hi_made, t + 1)
                dve.tensor_tensor(hwT_lo[:, t % 2, :], attended[t % 2][:, 0:P], hwT_hi[:, t % 2, :].bitcast(F32),
                                  ALU.subtract).then_inc(hw_lo_made, 1)

            def finish(t):
                dve.wait_ge(delta_added, t + 1)
                after(dve.tensor_tensor(acc[:, t, :], proj[t % 2][:, :], b_base_sb[:, :], ALU.add))
                dve.scalar_tensor_tensor(out=acc[:, t, :], in0=acc[:, t, :], scalar=gates_tanh[:, 1:2],
                                         in1=stage[:, t // HALF, t % HALF, :], op0=ALU.mult,
                                         op1=ALU.add).then_inc(out_made, 1)

            norm_y(0)
            for t in range(B + 1):
                if t + 1 < B:
                    norm_y(t + 1)
                if t < B:
                    y_lo(t)
                if t >= 1:
                    route_tile(t - 1)
                    hw_lo(t - 1)
                    finish(t - 1)

        @block.tensor
        def _(pe):
            def product(to, left, right, start=True, stop=True):
                n = len(left)
                for i, ((lh, ll), (rh, rl)) in enumerate(zip(left, right)):
                    pe.matmul(to, lh, rh, start=(start and i == 0), stop=False)
                    pe.matmul(to, lh, rl, start=False, stop=False)
                    ins = pe.matmul(to, ll, rh, start=False, stop=(stop and i == n - 1))
                return ins

            def chunks(hi, lo):
                return [(hi[:, c, :], lo[:, c, :]) for c in range(C)]

            def project_v(t):
                at = slice(t * P, (t + 1) * P)
                product(proj[t % 2][:, :], chunks(ctxT_hi[:, :, at], ctxT_lo[:, :, at]),
                        chunks(wv_hi, wv_lo)).then_inc(v_projected, 1)

            def turn_x(t):
                pe.wait_ge(x_normed, t + 1)
                if t >= 2:
                    pe.wait_ge(x_lo_made, t - 1)
                for c in range(C):
                    ins = pe.transpose(turned[t % 2][:, c * P:(c + 1) * P], x_norm[t % HALF][:, c, :], ident[:, :])
                ins.then_inc(x_turned, 1)

            pe.wait_ge(ident_made, 2)
            pe.wait_ge(lo_made, C)
            for t in range(B):
                pe.wait_ge(ctx_lo_made, t + 1)
                if t >= 2:
                    pe.wait_ge(v_copied, t - 1)
                project_v(t)
                if t >= HALF:
                    turn_x(2 * (t - HALF))
                    turn_x(2 * (t - HALF) + 1)

            def project_qk(h, j):
                p = (j + 1) % 2
                for k, (w_hi, w_lo, x_hi, x_lo) in enumerate(((wq_hi, wq_lo, xT_hi, xT_lo),
                                                              (wk_hi, wk_lo, ctxT_hi, ctxT_lo))):
                    pe.wait_ge(lo_made, split_q(h) + k)
                    for half in range(2):
                        if k == 1:
                            pe.wait_ge(qk_copied, 4 * h + half + 1)
                        elif is_first(h):
                            pe.wait_ge(x_lo_made, HALF * (half + 1))
                            pe.wait_ge(v_copied, B - 1 + half)
                        elif p == 1 and not (isinstance(h, int) and h == 1):
                            pe.wait_ge(out_added, 4 * (h - 3) + B - 1 + half)
                        else:
                            pe.wait_ge(qk_copied, 4 * (h - 1) + 3 + half)
                        at = slice(half * BANK, (half + 1) * BANK)
                        product(proj[half][:, :], chunks(w_hi[:, p, :, :], w_lo[:, p, :, :]),
                                chunks(x_hi[:, :, at], x_lo[:, :, at])).then_inc(qk_projected, 1)

            def make_scores(h):
                for half in range(2):
                    pe.wait_ge(qk_copied, 4 * h + 3 + half)
                    if not is_first(h):
                        pe.wait_ge(scores_biased, 2 * (h - 1) + half + 1)
                    for b in range(HALF * half, HALF * (half + 1)):
                        at = slice(b * P, (b + 1) * P)
                        ins = pe.matmul(score[half][:, (b % HALF) * P:(b % HALF + 1) * P], qT[:, at], kT[:, at],
                                        start=True, stop=True)
                    ins.then_inc(scores_made, 1)

            def turn_probs(h):
                for half in range(2):
                    pe.wait_ge(probs_scaled, 2 * h + half + 1)
                    if not is_first(h):
                        pe.wait_ge(probsT_copied, 2 * (h - 1) + half + 1)
                    for b in range(HALF * half, HALF * (half + 1)):
                        ins = pe.transpose(turned[half][:, (b % HALF) * P:(b % HALF + 1) * P], probs[:, b, :],
                                           ident[:, :])
                    ins.then_inc(probs_turned, 1)

            def attend(h, j):
                for half in range(2):
                    pe.wait_ge(probsT_copied, 2 * h + half + 1)
                    if j == 0:
                        pe.wait_ge(v_copied, 2 * h + HALF * (half + 1))
                    if not is_first(h):
                        pe.wait_ge(attn_lo_made, 2 * (h - 1) + half + 1)
                    for b in range(HALF * half, HALF * (half + 1)):
                        ins = pe.matmul(attended[half][:, (b % HALF) * P:(b % HALF + 1) * P],
                                        v[:, b, j * P:(j + 1) * P], probsT[:, b, :], start=True, stop=True)
                    ins.then_inc(attn_made, 1)

            def project_out(h, j):
                pe.wait_ge(lo_made, split_before(h) + 1)
                for t in range(B):
                    if t % HALF == 0:
                        pe.wait_ge(attn_lo_made, 2 * h + t // HALF + 1)
                    if t >= 2:
                        pe.wait_ge(out_added, 4 * (h - 1) + t - 1)
                    elif is_last(h):
                        pass
                    elif j == GH - 1:
                        pe.wait_ge(v_copied, 2 * (h + 1) + B - 1 + t)
                    else:
                        pe.wait_ge(qk_copied, 4 * (h + 1) + 3 + t)
                    at = slice(t * P, (t + 1) * P)
                    product(proj[t % 2][:, :], [(attn_hi[:, i, at], attn_lo[:, i, at]) for i in range(2)],
                            [(wo_hi[:, i, :], wo_lo[:, i, :]) for i in range(2)]).then_inc(out_projected, 1)

            def step(h, j):
                before = isinstance(h, int) and h < 0
                if not is_last(h):
                    project_qk(h + 1, j)
                if not before:
                    turn_probs(h)
                if not is_last(h):
                    make_scores(h + 1)
                if not before:
                    attend(h, j)
                    if j == GH - 1 and not is_last(h):
                        pe.wait_ge(lo_made, split_before(h) + 2)
                        for t in range(B):
                            if t < 2:
                                pe.wait_ge(qk_copied, 4 * (h + 1) + 3 + t)
                            else:
                                pe.wait_ge(v_copied, 2 * (h + 1) + t - 1)
                            project_v(t)
                    if j % 2 == 1:
                        project_out(h, j)

            step(-1, 3)
            run_steps(pe, step)

            def turn_y(t):
                pe.wait_ge(y_made, t + 1)
                if t >= 2:
                    pe.wait_ge(y_lo_made, t - 1)
                for c in range(C):
                    ins = pe.transpose(score[t % 2][:, c * P:(c + 1) * P], acc[:, t, c * P:(c + 1) * P], ident[:, :])
                ins.then_inc(y_turned, 1)

            def project_y(t):
                at = slice((t % 2) * P, (t % 2 + 1) * P)
                y = chunks(xT_hi[:, :, at], xT_lo[:, :, at])
                pe.wait_ge(y_lo_made, t + 1)
                if t >= 2:
                    pe.wait_ge(hw_made, t - 1)
                product(turned[t % 2][:, 0:AG], y, chunks(ag_hi, ag_lo)).then_inc(ag_projected, 1)
                if t >= 2:
                    pe.wait_ge(out_made, t - 1)
                else:
                    pe.wait_ge(out_added, 4 * (LAST - 1) + B - 1 + t)
                product(proj[t % 2][:, :], y, chunks(wv_hi, wv_lo), stop=False).then_inc(base_projected, 1)

            def add_delta(t):
                pe.wait_ge(hw_made, t + 1)
                if t >= 2:
                    pe.wait_ge(hw_lo_made, t - 1)
                pe.transpose(attended[t % 2][:, 0:P], hw[:, t % 2, :], ident[:, :]).then_inc(hw_turned, 1)
                pe.wait_ge(hw_lo_made, t + 1)
                product(proj[t % 2][:, :], [(hwT_hi[:, t % 2, :], hwT_lo[:, t % 2, :])], [(wb_hi, wb_lo)],
                        start=False).then_inc(delta_added, 1)

            pe.wait_ge(lo_made, split_before(H))
            turn_y(0)
            for t in range(B + 1):
                if t + 1 < B:
                    turn_y(t + 1)
                if t < B:
                    project_y(t)
                if t >= 1:
                    add_delta(t - 1)


def kernel(x, ctx_4096, mask_BxSxS2_bk0, g_xattn, g_ffn, L0_xattn_position_bias, L0_xattn_ln_weight, L0_xattn_w_q,
           L0_xattn_w_k, L0_xattn_w_v, L0_xattn_w_out, L0_ffn_W_base, L0_ffn_b_base, L0_ffn_W_gate, L0_ffn_A,
           L0_ffn_B):
    import numpy as np
    import concourse.bacc as bacc
    from concourse.bass_utils import run_bass_kernel_spmd

    def by_head(w):
        return np.asarray(w).reshape(H, P, C, P).transpose(0, 3, 2, 1).reshape(H, P, D)

    ag = np.concatenate([np.asarray(L0_ffn_A).reshape(ER, D), np.asarray(L0_ffn_W_gate)], axis=0)
    laid = {
        "x": x,
        "ctx": np.asarray(ctx_4096).reshape(B, P, C, P).transpose(3, 0, 2, 1).reshape(P, B, D),
        "mask": np.asarray(mask_BxSxS2_bk0).transpose(1, 0, 2),
        "gates": np.concatenate([np.asarray(g_xattn), np.asarray(g_ffn)]),
        "bias": L0_xattn_position_bias,
        "ln_w": np.asarray(L0_xattn_ln_weight).reshape(C, P).T,
        "w_q": by_head(L0_xattn_w_q),
        "w_k": by_head(L0_xattn_w_k),
        "w_v": np.asarray(L0_xattn_w_v).reshape(G, GH * P, C, P).transpose(0, 2, 3, 1).reshape(G * C, P, GH * P),
        "w_o": np.asarray(L0_xattn_w_out).T.reshape(H, P, D),
        "w_base": np.asarray(L0_ffn_W_base).T.reshape(C, P, D),
        "b_base": L0_ffn_b_base,
        "w_ag": ag.reshape(AG, C, P).transpose(2, 1, 0).reshape(P, C * AG),
        "w_b": np.asarray(L0_ffn_B).transpose(0, 2, 1).reshape(ER, D),
    }
    nc = bacc.Bacc("TRN2", target_bir_lowering=False, num_devices=1)
    arrays, args = {}, []
    for name, a in laid.items():
        a = np.ascontiguousarray(a)
        arrays[f"in_{name}"] = a
        args.append(nc.dram_tensor(f"in_{name}", a.shape, mybir.dt.from_np(a.dtype), kind="ExternalInput").ap())
    args.append(nc.dram_tensor("out_dram", (B, P, D), F32, kind="ExternalOutput").ap())
    program(nc, *args)
    r = run_bass_kernel_spmd(nc, [arrays], core_ids=[0])
    return r.results[0]["out_dram"]
```

```python
from contextlib import ExitStack

import concourse.bass as bass
from concourse import mybir

ALU = mybir.AluOpType
ACT = mybir.ActivationFunctionType
F32 = mybir.dt.float32
F32R = mybir.dt.float32r
U8 = mybir.dt.uint8
U32 = mybir.dt.uint32
AX_X = mybir.AxisListType.X

P = 128
B = 8
D = 512
C = D // P
H = 32
GH = 4
G = H // GH
T = B * P
HALF = B // 2
E = 8
R = 16
ER = E * R
AG = ER + E
EPS = 1e-5
MASKED = -1e30
LAST = H - 1
BANK = 512



def split_before(h):
    return 4 * h + 4 - (1 if isinstance(h, int) and h == H - 1 else 2 if isinstance(h, int) and h == H else 0)


def split_k(h):
    if isinstance(h, int) and h < 2:
        return 1 + 2 * h
    return split_before(h - 2) + 3


def stage_count(n, parity):
    fewer = 16 if isinstance(n, int) and n >= H - 2 else 0
    return 32 * n + (128 if parity == 0 else 32) - fewer


def bias_count(h, parity):
    return 8 * h + (16 if parity == 0 else 8)


def program(nc, x, ctx, mask, gates, bias, ln_w, w_q, w_k, w_v, w_o, w_base, b_base, w_ag, w_b, out):
    with ExitStack() as stack:
        def sb(name, shape, dt=F32):
            return stack.enter_context(nc.sbuf_tensor(name, shape, dt))

        def pb(name):
            return stack.enter_context(nc.psum_tensor(name, [P, BANK], F32))

        def sem(name):
            return stack.enter_context(nc.semaphore(name))

        xT_hi, xT_lo = sb("xT_hi", [P, C, T], F32R), sb("xT_lo", [P, C, T], F32R)
        ctxT_hi, ctxT_lo = sb("ctxT_hi", [P, C, T], F32R), sb("ctxT_lo", [P, C, T], F32R)
        acc = sb("acc", [P, B, D])
        wq_hi, wq_lo = sb("wq_hi", [P, 2, C, P], F32R), sb("wq_lo", [P, 2, C, P], F32R)
        wk_hi, wk_lo = sb("wk_hi", [P, 2, C, P], F32R), sb("wk_lo", [P, 2, C, P], F32R)
        wv_hi, wv_lo = sb("wv_hi", [P, C, GH * P], F32R), sb("wv_lo", [P, C, GH * P], F32R)
        wo_hi, wo_lo = sb("wo_hi", [P, 2, D], F32R), sb("wo_lo", [P, 2, D], F32R)
        ag_hi, ag_lo = sb("ag_hi", [P, C, AG], F32R), sb("ag_lo", [P, C, AG], F32R)
        stage = sb("stage", [P, 2, 4, D])
        qT, kT = sb("qT", [P, T]), sb("kT", [P, T])
        v = sb("v", [P, B, GH * P])
        probs, probsT = sb("probs", [P, B, P]), sb("probsT", [P, B, P])
        attn_hi, attn_lo = sb("attn_hi", [P, 2, T], F32R), sb("attn_lo", [P, 2, T], F32R)
        pos_bias = sb("pos_bias", [P, 2, P])
        mask8 = sb("mask8", [P, B, P], U8)
        mask_bias, full_bias = sb("mask_bias", [P, B, P]), sb("full_bias", [P, B, P])
        row_any, row_scale = sb("row_any", [P, B]), sb("row_scale", [P, B])
        neg_max, sums, sums_inv, prob_scale = (sb(n, [P, B]) for n in ("neg_max", "sums", "sums_inv", "prob_scale"))
        ident = sb("ident", [P, P])
        ln_w_sb = sb("ln_w_sb", [P, C])
        gates_sb, gates_tanh = sb("gates_sb", [P, 2]), sb("gates_tanh", [P, 2])
        b_base_sb = sb("b_base_sb", [P, D])
        x_factor, x_shift = sb("x_factor", [P, B]), sb("x_shift", [P, B])
        y_shift = sb("y_shift", [P, B])
        half_neg = sb("half_neg", [P, B])
        experts = sb("experts", [P, E])
        stats, moments = sb("stats", [P, B, 6]), sb("moments", [P, B, 2])
        var_eps, rstd, rms_in, rms_inv, x_scale = (
            sb(n, [P, B]) for n in ("var_eps", "rstd", "rms_in", "rms_inv", "x_scale"))
        logits, top8, top_i = sb("logits", [P, 2, E]), sb("top8", [P, 2, 8]), sb("top_i", [P, 2, 8], U32)
        top_f = sb("top_f", [P, 2, 2])
        gap, ratio, ratio1, w_first, w_second = (
            sb(n, [P, 2]) for n in ("gap", "ratio", "ratio1", "w_first", "w_second"))
        route1, route2, route = (sb(n, [P, 2, E]) for n in ("route1", "route2", "route"))
        hw = sb("hw", [P, 2, ER])
        hwT_hi, hwT_lo = sb("hwT_hi", [P, 2, P], F32R), sb("hwT_lo", [P, 2, P], F32R)

        y_norm = [stage[:, t // HALF, t % HALF, :] for t in range(B)]
        wb_hi = wq_hi[:, 0, :, :].rearrange("p c n -> p (c n)")
        wb_lo = wq_lo[:, 0, :, :].rearrange("p c n -> p (c n)")
        ag_raw = stage[:, 0, 2:4, :].rearrange("p a n -> p (a n)")[:, 0:C * AG]
        x_norm = [buf[:, HALF * i:HALF * (i + 1), :] for buf in (probs, probsT, full_bias) for i in range(2)]
        x_norm += [qT[:, i * BANK:(i + 1) * BANK].rearrange("p (c n) -> p c n", c=C) for i in range(2)]
        ctx_raw = [v[:, b, :].rearrange("p (c t) -> p c t", c=C) for b in range(B)]

        proj = [pb("proj0"), pb("proj1")]
        score = [pb("score0"), pb("score1")]
        turned = [pb("turned0"), pb("turned1")]
        attended = [pb("attended0"), pb("attended1")]

        stage_loaded = [sem("stage_loaded0"), sem("stage_loaded1")]
        bias_loaded = [sem("bias_loaded0"), sem("bias_loaded1")]
        first_v_loaded = [sem(f"first_v_loaded{c}") for c in range(C)]
        ctx_loaded = [sem(f"ctx_loaded{b}") for b in range(B)]
        x_loaded = [sem("x_loaded0"), sem("x_loaded1")]
        small_loaded = sem("small_loaded")
        out_stored = sem("out_stored")
        hi_made, lo_made = sem("hi_made"), sem("lo_made")
        ident_made, consts_made, mask_made, mask_chain = (
            sem(n) for n in ("ident_made", "consts_made", "mask_made", "mask_chain"))
        first_v_hi_made, first_v_lo_made = sem("first_v_hi_made"), sem("first_v_lo_made")
        ctx_hi_made, ctx_lo_made = sem("ctx_hi_made"), sem("ctx_lo_made")
        ln_chain, ln_pow = sem("ln_chain"), sem("ln_pow")
        x_normed, x_turned, x_hi_made, x_lo_made = (
            sem(n) for n in ("x_normed", "x_turned", "x_hi_made", "x_lo_made"))
        h_made, tanh_made = sem("h_made"), sem("tanh_made")
        bias_scaled = sem("bias_scaled")
        qk_projected, qk_copied = sem("qk_projected"), sem("qk_copied")
        v_projected, v_copied = sem("v_projected"), sem("v_copied")
        bias_made = sem("bias_made")
        scores_made, scores_biased, max_made = sem("scores_made"), sem("scores_biased"), sem("max_made")
        exp_made, sums_inverted, scale_made = sem("exp_made"), sem("sums_inverted"), sem("scale_made")
        probs_scaled, probs_turned, probsT_copied = (
            sem(n) for n in ("probs_scaled", "probs_turned", "probsT_copied"))
        attn_made, attn_hi_made, attn_lo_made = sem("attn_made"), sem("attn_hi_made"), sem("attn_lo_made")
        out_projected, out_added = sem("out_projected"), sem("out_added")
        x1_made, f_chain, f_var, f_pow = sem("x1_made"), sem("f_chain"), sem("f_var"), sem("f_pow")
        y_made, y_turned, y_hi_made, y_lo_made = (
            sem(n) for n in ("y_made", "y_turned", "y_hi_made", "y_lo_made"))
        ag_projected, base_projected = sem("ag_projected"), sem("base_projected")
        gap_made, ratio_made, hw_made, hw_turned = (
            sem(n) for n in ("gap_made", "ratio_made", "hw_made", "hw_turned"))
        hw_hi_made, hw_lo_made, delta_added = sem("hw_hi_made"), sem("hw_lo_made"), sem("delta_added")
        x1_shifted, out_made = sem("x1_shifted"), sem("out_made")

        def run_steps(eng, step):
            for h in range(GH):
                step(h, h % GH)
            with eng.Fori(1, G - 1) as g:
                for j in range(GH):
                    step(g * GH + j, j)
            for h in range(H - GH, H):
                step(h, h % GH)

        def is_last(h):
            return isinstance(h, int) and h == LAST

        def is_first(h):
            return isinstance(h, int) and h == 0

        def pieces(h, j):
            raw = [stage[:, j % 2, i, :] for i in range(4)]
            four = [r.rearrange("p (c n) -> p c n", c=C) for r in raw]
            p = j % 2
            found = [(wo_hi[:, p, :], wo_lo[:, p, :], raw[0]), (wv_hi[:, j, :], wv_lo[:, j, :], raw[1])]
            if not isinstance(h, int) or h + 2 <= LAST:
                found += [(wk_hi[:, p, :, :], wk_lo[:, p, :, :], four[2]),
                          (wq_hi[:, p, :, :], wq_lo[:, p, :, :], four[3])]
            elif h == LAST - 1:
                found.append((ag_hi[:, :, :], ag_lo[:, :, :], ag_raw.rearrange("p (c n) -> p c n", c=C)))
            else:
                found.append((wb_hi, wb_lo, raw[2]))
            return found

        first_v = [(wv_hi[:, c, :], wv_lo[:, c, :], stage[:, 1, c, :]) for c in range(C)]
        first_qk = []
        for i in range(2):
            for k, (hi, lo) in enumerate(((wk_hi, wk_lo), (wq_hi, wq_lo))):
                raw = stage[:, 0, 2 * i + k, :].rearrange("p (c n) -> p c n", c=C)
                first_qk.append((hi[:, i, :, :], lo[:, i, :, :], raw))

        block = stack.enter_context(nc.Block())

        @block.sync
        def _(sp):
            def load_first(c, tiles):
                sp.dma_start(stage[:, 1, c, :], w_v[c, :, :]).then_inc(first_v_loaded[c], 16)
                for b in tiles:
                    sp.dma_start(v[:, b, :], ctx[:, b, :]).then_inc(ctx_loaded[b], 16)

            load_first(0, [0])
            load_first(1, [])
            load_first(2, [])
            load_first(3, [1, 2, 3])
            sp.dma_start(mask8[:, :, :], mask).then_inc(small_loaded, 16)
            sp.dma_start(ln_w_sb[:, :], ln_w).then_inc(small_loaded, 16)
            sp.dma_start(gates_sb[:, :], gates.partition_broadcast(P)).then_inc(small_loaded, 16)
            sp.dma_start(b_base_sb[:, :], b_base.partition_broadcast(P)).then_inc(small_loaded, 16)

            def load_x(i):
                sp.dma_start(acc[:, HALF * i:HALF * (i + 1), :],
                             x[HALF * i:HALF * (i + 1), :, :].rearrange("b p d -> p b d")).then_inc(x_loaded[i], 16)

            load_x(0)
            for b in range(4, B):
                sp.dma_start(v[:, b, :], ctx[:, b, :]).then_inc(ctx_loaded[b], 16)
            load_x(1)
            for i in range(2):
                sp.dma_start(stage[:, 0, 2 * i, :], w_k[i, :, :]).then_inc(stage_loaded[0], 16)
                sp.dma_start(stage[:, 0, 2 * i + 1, :], w_q[i, :, :]).then_inc(stage_loaded[0], 16)
            for i in range(2):
                sp.dma_start(pos_bias[:, i, :], bias[i, :, :]).then_inc(bias_loaded[i], 16)

            def step(n, j):
                p = j % 2
                if isinstance(n, int) and n == 1:
                    sp.wait_ge(first_v_lo_made, C)
                else:
                    sp.wait_ge(lo_made, 4 if isinstance(n, int) and n == 0 else split_before(n - 1))
                sp.dma_start(stage[:, p, 0, :], w_o[n, :, :]).then_inc(stage_loaded[p], 16)
                wide = w_base[j, :, :] if isinstance(n, int) and n >= H - GH else w_v[n + GH, :, :]
                sp.dma_start(stage[:, p, 1, :], wide).then_inc(stage_loaded[p], 16)
                if not isinstance(n, int) or n + 2 <= LAST:
                    sp.dma_start(stage[:, p, 2, :], w_k[n + 2, :, :]).then_inc(stage_loaded[p], 16)
                    sp.dma_start(stage[:, p, 3, :], w_q[n + 2, :, :]).then_inc(stage_loaded[p], 16)
                elif n == LAST - 1:
                    sp.dma_start(ag_raw, w_ag).then_inc(stage_loaded[p], 16)
                else:
                    sp.dma_start(stage[:, p, 2, :], w_b).then_inc(stage_loaded[p], 16)
                if not isinstance(n, int) or n + 2 <= LAST:
                    sp.wait_ge(bias_made, n + 1)
                    sp.dma_start(pos_bias[:, p, :], bias[n + 2, :, :]).then_inc(bias_loaded[p], 16)

            run_steps(sp, step)

            for t in range(B):
                sp.wait_ge(out_made, t + 1)
                sp.dma_start(out[t, :, :], acc[:, t, :]).then_inc(out_stored, 16)
            sp.wait_ge(out_stored, 16 * B)

        @block.gpsimd
        def _(pool):
            pool.memset(ident[:, :], 0.0).then_inc(ident_made, 1)
            pool.memset(half_neg[:, :], -0.5).then_inc(consts_made, 1)
            for e in range(E):
                pool.memset(experts[:, e:e + 1], float(e)).then_inc(consts_made, 1)
            pool.wait_ge(ident_made, 1)
            pool.affine_select(out=ident[:, :], in_=ident[:, :], compare_op=ALU.not_equal, fill=1.0,
                               base=0, pattern=[[-1, P]], channel_multiplier=1).then_inc(ident_made, 1)
            pool.wait_ge(consts_made, 1 + E)

            def make_lo(piece, n):
                hi, lo, raw = piece
                pool.wait_ge(hi_made, n)
                pool.tensor_tensor(lo, raw, hi.bitcast(F32), ALU.subtract).then_inc(lo_made, 1)

            for half in range(2):
                a, b = HALF * half, HALF * (half + 1)
                pool.wait_ge(ln_chain, 4 * half + 1)
                pool.tensor_tensor(rstd[:, a:b], var_eps[:, a:b], half_neg[:, a:b], ALU.pow).then_inc(ln_pow, 1)
                pool.wait_ge(ln_chain, 4 * half + 4)
                pool.tensor_tensor(rms_inv[:, a:b], rms_in[:, a:b], half_neg[:, a:b], ALU.pow).then_inc(ln_pow, 1)
            for i, piece in enumerate(first_qk):
                make_lo(piece, 1 + i)

            def add_bias(h, j):
                p = j % 2
                pool.wait_ge(bias_loaded[p], bias_count(h, p))
                if is_first(h):
                    pool.wait_ge(mask_made, 1)
                    pool.wait_ge(x_turned, B)
                else:
                    pool.wait_ge(scores_biased, 2 * h)
                pool.tensor_tensor(full_bias[:, :, :], mask_bias[:, :, :],
                                   pos_bias[:, p, :].unsqueeze(1).broadcast_to([P, B, P]),
                                   ALU.add).then_inc(bias_made, 1)

            add_bias(0, 0)

            def scale_probs(h):
                for half in range(2):
                    a, b = HALF * half, HALF * (half + 1)
                    pool.wait_ge(scale_made, 2 * h + half + 1)
                    pool.tensor_tensor(probs[:, a:b, :], probs[:, a:b, :],
                                       prob_scale[:, a:b].unsqueeze(2).broadcast_to([P, HALF, P]),
                                       ALU.mult).then_inc(probs_scaled, 1)

            def step(h, j):
                for i, piece in enumerate(pieces(h, j)):
                    make_lo(piece, split_before(h) + 1 + i)
                if not is_last(h):
                    scale_probs(h + 1)
                if not isinstance(h, int) or h + 2 <= LAST:
                    add_bias(h + 2, j)

            scale_probs(0)
            add_bias(1, 1)
            run_steps(pool, step)

            pool.wait_ge(tanh_made, 1)
            pool.tensor_scalar(b_base_sb[:, :], b_base_sb[:, :], gates_tanh[:, 1:2], None, ALU.mult).then_inc(bias_scaled, 1)
            pool.wait_ge(bias_scaled, 1)
            for t in range(B + 1):
                if t < B:
                    one = slice(t, t + 1)
                    pool.wait_ge(f_var, t + 1)
                    pool.tensor_tensor(rstd[:, one], var_eps[:, one], half_neg[:, one], ALU.pow).then_inc(f_pow, 1)
                    pool.wait_ge(f_pow, 2 * t + 1)
                    pool.tensor_scalar(y_shift[:, one], moments[:, t, 0:1], rstd[:, one], -1.0,
                                       ALU.mult, ALU.mult).then_inc(f_pow, 1)
                if t >= 1:
                    pool.wait_ge(y_made, t)
                    pool.tensor_tensor(acc[:, t - 1, :], acc[:, t - 1, :], b_base_sb[:, :], ALU.add).then_inc(x1_shifted, 1)

        @block.scalar
        def _(act):
            def make_hi(piece):
                hi, _, raw = piece
                act.activation(hi, raw, ACT.Copy).then_inc(hi_made, 1)

            def copy_v(g, t):
                act.wait_ge(v_projected, B * g + t + 1)
                if not (isinstance(g, int) and g == 0):
                    act.wait_ge(attn_made, 2 * (GH * g - 1) + t // HALF + 1)
                act.activation(v[:, t, :], proj[t % 2][:, :], ACT.Copy).then_inc(v_copied, 1)

            def first_v_hi(c):
                act.wait_ge(first_v_loaded[c], 16)
                act.activation(first_v[c][0], first_v[c][2], ACT.Copy).then_inc(first_v_hi_made, 1)

            def ctx_hi(b):
                act.wait_ge(ctx_loaded[b], 16)
                act.activation(ctxT_hi[:, :, b * P:(b + 1) * P], ctx_raw[b], ACT.Copy).then_inc(ctx_hi_made, 1)

            def x_hi(b):
                act.wait_ge(x_turned, b + 1)
                for c in range(C):
                    ins = act.activation(xT_hi[:, c, b * P:(b + 1) * P], turned[b % 2][:, c * P:(c + 1) * P],
                                         ACT.Identity, scale=ln_w_sb[:, c:c + 1])
                ins.then_inc(x_hi_made, 1)

            first_v_hi(0)
            ctx_hi(0)
            for c in range(1, C):
                first_v_hi(c)
            for b in range(1, B):
                ctx_hi(b)
                if b >= 3:
                    copy_v(0, b - 3)
                if b == 3:
                    act.wait_ge(small_loaded, 16 * 4)
                    act.activation(gates_tanh[:, :], gates_sb[:, :], ACT.Tanh).then_inc(tanh_made, 1)
            act.wait_ge(stage_loaded[0], 16 * C)
            for piece in first_qk:
                make_hi(piece)
            for i, t in enumerate(range(B - 3, B)):
                copy_v(0, t)
                x_hi(2 * i)
                x_hi(2 * i + 1)
            x_hi(6)
            x_hi(7)

            def copy_kq(h, k, half):
                act.wait_ge(qk_projected, 4 * h + 2 * k + half + 1)
                if not is_first(h):
                    act.wait_ge(scores_made, 2 * (h - 1) + half + 1)
                act.activation((kT, qT)[k][:, half * BANK:(half + 1) * BANK], proj[half][:, :],
                               ACT.Copy).then_inc(qk_copied, 1)

            def exp_scores(h):
                for half in range(2):
                    act.wait_ge(max_made, 2 * h + half + 1)
                    for b in range(HALF * half, HALF * (half + 1)):
                        ins = act.activation(probs[:, b, :], probs[:, b, :], ACT.Exp, bias=neg_max[:, b:b + 1],
                                             scale=1.0, accum_out=sums[:, b:b + 1])
                    ins.then_inc(exp_made, 1)

            def step(h, j):
                found = pieces(h, j)
                if not is_last(h):
                    copy_kq(h + 1, 0, 0)
                act.wait_ge(stage_loaded[j % 2], stage_count(h, j % 2))
                if j % 2 == 0 and not is_first(h):
                    act.wait_ge(out_projected, 4 * h)
                make_hi(found[0])
                if j == 0:
                    act.wait_ge(v_projected, 2 * h + B)
                make_hi(found[1])
                if not is_last(h):
                    copy_kq(h + 1, 0, 1)
                for piece in found[2:]:
                    make_hi(piece)
                if not is_last(h):
                    copy_kq(h + 1, 1, 0)
                    copy_kq(h + 1, 1, 1)
                for half in range(2):
                    act.wait_ge(probs_turned, 2 * h + half + 1)
                    if not is_first(h):
                        act.wait_ge(attn_made, 2 * (h - 1) + half + 1)
                    act.activation(probsT[:, HALF * half:HALF * (half + 1), :], turned[half][:, :],
                                   ACT.Copy).then_inc(probsT_copied, 1)
                for half in range(2):
                    act.wait_ge(attn_made, 2 * h + half + 1)
                    if j % 2 == 0 and half == 0 and not is_first(h):
                        act.wait_ge(out_projected, 4 * h)
                    act.activation(attn_hi[:, j % 2, half * BANK:(half + 1) * BANK], attended[half][:, :],
                                   ACT.Copy).then_inc(attn_hi_made, 1)
                if not is_last(h):
                    exp_scores(h + 1)
                if j == GH - 1 and not is_last(h):
                    for t in range(B):
                        copy_v_next(h, t)

            def copy_v_next(h, t):
                act.wait_ge(v_projected, 2 * (h + 1) + t + 1)
                act.wait_ge(attn_made, 2 * h + t // HALF + 1)
                act.activation(v[:, t, :], proj[t % 2][:, :], ACT.Copy).then_inc(v_copied, 1)

            for k in range(2):
                for half in range(2):
                    copy_kq(0, k, half)
            exp_scores(0)
            run_steps(act, step)

            def y_and_round(t):
                if t + 1 < B:
                    act.wait_ge(f_pow, 2 * (t + 1) + 2)
                    act.activation(y_norm[t + 1], acc[:, t + 1, :], ACT.Identity, bias=y_shift[:, t + 1:t + 2],
                                   scale=rstd[:, t + 1:t + 2]).then_inc(y_made, 1)

            def y_hi(t):
                act.wait_ge(y_turned, t + 1)
                if t >= 2:
                    act.wait_ge(base_projected, t - 1)
                act.activation(xT_hi[:, :, (t % 2) * P:(t % 2 + 1) * P],
                               attended[t % 2][:, :].rearrange("p (c t) -> p c t", c=C),
                               ACT.Copy).then_inc(y_hi_made, 1)

            act.wait_ge(lo_made, split_before(H))
            y_and_round(-1)
            for t in range(-1, B + 1):
                if t + 1 < B:
                    y_hi(t + 1)
                if t + 2 < B and t >= -1:
                    y_and_round(t + 1)
                if t >= 1:
                    u = t - 1
                    act.wait_ge(hw_turned, u + 1)
                    if u >= 2:
                        act.wait_ge(delta_added, u - 1)
                    act.activation(hwT_hi[:, u % 2, :], turned[u % 2][:, 2 * P:3 * P], ACT.Copy).then_inc(hw_hi_made, 1)
                if 0 <= t < B:
                    act.wait_ge(gap_made, t + 1)
                    act.activation(ratio[:, t % 2:t % 2 + 1], gap[:, t % 2:t % 2 + 1], ACT.Exp).then_inc(ratio_made, 1)

        @block.vector
        def _(dve):
            def first_v_lo(c):
                hi, lo, raw = first_v[c]
                dve.wait_ge(first_v_hi_made, c + 1)
                dve.tensor_tensor(lo, raw, hi.bitcast(F32), ALU.subtract).then_inc(first_v_lo_made, 1)

            def ctx_lo(b):
                dve.wait_ge(ctx_hi_made, b + 1)
                at = slice(b * P, (b + 1) * P)
                dve.tensor_tensor(ctxT_lo[:, :, at], ctx_raw[b], ctxT_hi[:, :, at].bitcast(F32),
                                  ALU.subtract).then_inc(ctx_lo_made, 1)

            def norm_x(half):
                a, b = HALF * half, HALF * (half + 1)
                dve.wait_ge(x_loaded[half], 16)
                for t in range(a, b):
                    dve.bn_stats(stats[:, t, :], acc[:, t, :]).then_inc(f_chain, 1)
                dve.wait_ge(f_chain, 2 * b - HALF)
                for t in range(a, b):
                    dve.bn_aggr(moments[:, t, :], stats[:, t, :]).then_inc(f_chain, 1)
                dve.wait_ge(f_chain, 2 * b)
                mean, var = moments[:, a:b, 0], moments[:, a:b, 1]
                dve.tensor_scalar(var_eps[:, a:b], var, EPS, None, ALU.add).then_inc(ln_chain, 1)
                dve.wait_ge(ln_pow, 2 * half + 1)
                dve.tensor_tensor(rms_in[:, a:b], var, rstd[:, a:b], ALU.mult).then_inc(ln_chain, 1)
                dve.wait_ge(ln_chain, 4 * half + 2)
                dve.tensor_tensor(rms_in[:, a:b], rms_in[:, a:b], rstd[:, a:b], ALU.mult).then_inc(ln_chain, 1)
                dve.wait_ge(ln_chain, 4 * half + 3)
                dve.tensor_scalar(rms_in[:, a:b], rms_in[:, a:b], EPS, None, ALU.add).then_inc(ln_chain, 1)
                dve.wait_ge(ln_pow, 2 * half + 2)
                dve.tensor_tensor(x_scale[:, a:b], rstd[:, a:b], rms_inv[:, a:b], ALU.mult).then_inc(mask_chain, 1)
                dve.wait_ge(mask_chain, half + 1)
                for t in range(a, b):
                    dve.tensor_scalar(x_norm[t], acc[:, t, :].rearrange("p (c n) -> p c n", c=C),
                                      moments[:, t, 0:1], x_scale[:, t:t + 1],
                                      ALU.subtract, ALU.mult).then_inc(x_normed, 1)
                dve.wait_ge(x_normed, b)

            def begin_sums():
                dve.wait_ge(x_normed, B)
                dve.tensor_scalar(x_factor[:, :], rstd[:, :], gates_tanh[:, 0:1], None, ALU.mult).then_inc(h_made, 1)
                dve.wait_ge(h_made, 1)
                dve.tensor_tensor(x_shift[:, :], moments[:, :, 0], x_factor[:, :], ALU.mult).then_inc(h_made, 1)
                dve.wait_ge(h_made, 2)
                dve.tensor_scalar(x_factor[:, :], x_factor[:, :], 1.0, None, ALU.add).then_inc(h_made, 1)
                dve.wait_ge(h_made, 3)
                for t in range(B):
                    dve.tensor_scalar(acc[:, t, :], acc[:, t, :], x_factor[:, t:t + 1], x_shift[:, t:t + 1],
                                      ALU.mult, ALU.subtract).then_inc(h_made, 1)

            def x_lo(t):
                dve.wait_ge(x_hi_made, t + 1)
                for c in range(C):
                    at = slice(t * P, (t + 1) * P)
                    ins = dve.scalar_tensor_tensor(out=xT_lo[:, c, at], in0=turned[t % 2][:, c * P:(c + 1) * P],
                                                   scalar=ln_w_sb[:, c:c + 1], in1=xT_hi[:, c, at].bitcast(F32),
                                                   op0=ALU.mult, op1=ALU.subtract)
                ins.then_inc(x_lo_made, 1)

            first_v_lo(0)
            ctx_lo(0)
            for c in range(1, C):
                first_v_lo(c)
            for b in range(1, B):
                ctx_lo(b)
            norm_x(0)
            norm_x(1)
            dve.wait_ge(small_loaded, 16 * 4)
            dve.tensor_scalar(mask_bias[:, :, :], mask8[:, :, :], -MASKED, MASKED, ALU.mult, ALU.add).then_inc(mask_made, 1)
            dve.tensor_reduce(row_any[:, :], mask8[:, :, :], AX_X, ALU.max).then_inc(mask_made, 1)
            dve.wait_ge(tanh_made, 1)
            dve.wait_ge(mask_made, 2)
            dve.tensor_scalar(row_scale[:, :], row_any[:, :], gates_tanh[:, 0:1], None, ALU.mult).then_inc(mask_made, 1)
            for t in range(B):
                x_lo(t)
            begin_sums()

            def add_scores_bias(h, half):
                a, b = HALF * half, HALF * (half + 1)
                dve.wait_ge(scores_made, 2 * h + half + 1)
                dve.wait_ge(bias_made, h + 1)
                if not is_first(h):
                    dve.wait_ge(probs_turned, 2 * (h - 1) + half + 1)
                dve.tensor_tensor(probs[:, a:b, :], score[half][:, :].rearrange("p (b k) -> p b k", b=HALF),
                                  full_bias[:, a:b, :], ALU.add).then_inc(scores_biased, 1)

            def take_max(h, half):
                a, b = HALF * half, HALF * (half + 1)
                dve.wait_ge(scores_biased, 2 * h + half + 1)
                dve.tensor_reduce(neg_max[:, a:b], probs[:, a:b, :], AX_X, ALU.max, negate=True).then_inc(max_made, 1)

            def prob_scales(h, half):
                a, b = HALF * half, HALF * (half + 1)
                dve.wait_ge(exp_made, 2 * h + half + 1)
                dve.reciprocal(sums_inv[:, a:b], sums[:, a:b]).then_inc(sums_inverted, 1)
                dve.wait_ge(sums_inverted, 2 * h + half + 1)
                dve.tensor_tensor(prob_scale[:, a:b], sums_inv[:, a:b], row_scale[:, a:b], ALU.mult).then_inc(scale_made, 1)

            def attn_rest(h, j, half):
                dve.wait_ge(attn_hi_made, 2 * h + half + 1)
                at = slice(half * BANK, (half + 1) * BANK)
                dve.tensor_tensor(attn_lo[:, j % 2, at], attended[half][:, :],
                                  attn_hi[:, j % 2, at].bitcast(F32), ALU.subtract).then_inc(attn_lo_made, 1)

            def add_out(n, t):
                dve.wait_ge(out_projected, n + 1)
                dve.tensor_tensor(acc[:, t, :], proj[t % 2][:, :], acc[:, t, :], ALU.add).then_inc(out_added, 1)

            def step(h, j):
                if not is_last(h):
                    add_scores_bias(h + 1, 0)
                    take_max(h + 1, 0)
                    add_scores_bias(h + 1, 1)
                attn_rest(h, j, 0)
                if not is_last(h):
                    take_max(h + 1, 1)
                attn_rest(h, j, 1)
                scales_due = not is_last(h)
                if scales_due and (j % 2 == 0 or j == GH - 1) and not (isinstance(h, int) and h == LAST - 1):
                    prob_scales(h + 1, 0)
                    prob_scales(h + 1, 1)
                    scales_due = False
                if (j % 2 == 1 or isinstance(h, int) and h == LAST - 1) and not is_last(h):
                    n = 4 * h if isinstance(h, int) and h == LAST - 1 else 4 * (h - 1)
                    if isinstance(h, int) and h == 1:
                        dve.wait_ge(h_made, 3 + B)
                    else:
                        dve.wait_ge(out_added, n)
                    for t in range(B):
                        add_out(n + t, t)
                        if t in (1, 3) and scales_due:
                            prob_scales(h + 1, t // 2)

            add_scores_bias(0, 0)
            take_max(0, 0)
            add_scores_bias(0, 1)
            take_max(0, 1)
            prob_scales(0, 0)
            prob_scales(0, 1)
            run_steps(dve, step)

            def make_x1(t):
                dve.wait_ge(out_projected, 4 * H + t + 1)
                if t == 0:
                    dve.wait_ge(out_added, 4 * H)
                dve.tensor_tensor(acc[:, t, :], score[t % 2][:, :], acc[:, t, :], ALU.add).then_inc(x1_made, 1)
                dve.wait_ge(x1_made, t + 1)
                n = 2 * B + 2 * t
                dve.bn_stats(stats[:, t, :], acc[:, t, :]).then_inc(f_chain, 1)
                dve.wait_ge(f_chain, n + 1)
                dve.bn_aggr(moments[:, t, :], stats[:, t, :]).then_inc(f_chain, 1)
                dve.wait_ge(f_chain, n + 2)
                dve.tensor_scalar(var_eps[:, t:t + 1], moments[:, t, 1:2], EPS, None, ALU.add).then_inc(f_var, 1)

            def y_lo(t):
                dve.wait_ge(y_hi_made, t + 1)
                at = slice((t % 2) * P, (t % 2 + 1) * P)
                dve.tensor_tensor(xT_lo[:, :, at], attended[t % 2][:, :].rearrange("p (c t) -> p c t", c=C),
                                  xT_hi[:, :, at].bitcast(F32), ALU.subtract).then_inc(y_lo_made, 1)

            route_steps = [0]

            def after(ins):
                route_steps[0] += 1
                ins.then_inc(ln_chain, 1)
                dve.wait_ge(ln_chain, 2 * 4 + route_steps[0])

            def route_tile(t):
                p = t % 2
                one = slice(p, p + 1)
                dve.wait_ge(ag_projected, t + 1)
                after(dve.tensor_copy(logits[:, p, :], turned[p][:, ER:AG]))
                after(dve.max(top8[:, p, :], logits[:, p, :]))
                dve.tensor_tensor(gap[:, one], top8[:, p, 1:2], top8[:, p, 0:1], ALU.subtract).then_inc(gap_made, 1)
                after(dve.max_index(top_i[:, p, :], top8[:, p, :], logits[:, p, :]))
                after(dve.tensor_copy(top_f[:, p, :], top_i[:, p, 0:2]))
                dve.wait_ge(ratio_made, t + 1)
                after(dve.tensor_scalar(ratio1[:, one], ratio[:, one], 1.0, None, ALU.add))
                after(dve.reciprocal(w_first[:, one], ratio1[:, one]))
                after(dve.tensor_tensor(w_second[:, one], ratio[:, one], w_first[:, one], ALU.mult))
                dve.tensor_scalar(route1[:, p, :], experts[:, :], top_f[:, p, 0:1], w_first[:, one],
                                  ALU.is_equal, ALU.mult)
                after(dve.tensor_scalar(route2[:, p, :], experts[:, :], top_f[:, p, 1:2], w_second[:, one],
                                        ALU.is_equal, ALU.mult))
                after(dve.tensor_tensor(route[:, p, :], route1[:, p, :], route2[:, p, :], ALU.add))
                dve.tensor_tensor(hw[:, p, :].rearrange("p (e r) -> p e r", e=E),
                                  turned[p][:, 0:ER].rearrange("p (e r) -> p e r", e=E),
                                  route[:, p, :].unsqueeze(2).broadcast_to([P, E, R]), ALU.mult).then_inc(hw_made, 1)

            def hw_lo(t):
                dve.wait_ge(hw_hi_made, t + 1)
                dve.tensor_tensor(hwT_lo[:, t % 2, :], turned[t % 2][:, 2 * P:3 * P], hwT_hi[:, t % 2, :].bitcast(F32),
                                  ALU.subtract).then_inc(hw_lo_made, 1)

            def finish(t):
                dve.wait_ge(delta_added, t + 1)
                dve.wait_ge(x1_shifted, t + 1)
                dve.scalar_tensor_tensor(out=acc[:, t, :], in0=proj[t % 2][:, :], scalar=gates_tanh[:, 1:2],
                                         in1=acc[:, t, :], op0=ALU.mult, op1=ALU.add).then_inc(out_made, 1)

            make_x1(0)
            make_x1(1)
            y_lo(0)
            for t in range(B + 2):
                if t >= 2:
                    finish(t - 2)
                if t + 2 < B:
                    make_x1(t + 2)
                if t + 1 < B:
                    y_lo(t + 1)
                if 1 <= t <= B:
                    hw_lo(t - 1)
                if t < B:
                    route_tile(t)

        @block.tensor
        def _(pe):
            def product(to, left, right, start=True, stop=True, waits=None):
                n = len(left)
                waits = waits or {}
                for i, ((lh, ll), (rh, rl)) in enumerate(zip(left, right)):
                    if i in waits:
                        pe.wait_ge(*waits[i])
                    pe.matmul(to, lh, rh, start=(start and i == 0), stop=False)
                    pe.matmul(to, lh, rl, start=False, stop=False)
                    ins = pe.matmul(to, ll, rh, start=False, stop=(stop and i == n - 1))
                return ins

            def chunks(hi, lo):
                return [(hi[:, c, :], lo[:, c, :]) for c in range(C)]

            def project_v(t, waits=None):
                at = slice(t * P, (t + 1) * P)
                product(proj[t % 2][:, :], chunks(ctxT_hi[:, :, at], ctxT_lo[:, :, at]),
                        chunks(wv_hi, wv_lo), waits=waits).then_inc(v_projected, 1)

            def turn_x(t):
                pe.wait_ge(x_normed, t + 1)
                if t >= 2:
                    pe.wait_ge(x_lo_made, t - 1)
                for c in range(C):
                    ins = pe.transpose(turned[t % 2][:, c * P:(c + 1) * P], x_norm[t][:, c, :], ident[:, :])
                ins.then_inc(x_turned, 1)

            pe.wait_ge(ident_made, 2)
            for t in range(B):
                pe.wait_ge(ctx_lo_made, t + 1)
                if t >= 2:
                    pe.wait_ge(v_copied, t - 1)
                project_v(t, waits={c: (first_v_lo_made, c + 1) for c in range(C)} if t == 0 else None)
                if t >= B - 3:
                    turn_x(2 * (t - B + 3))
                    turn_x(2 * (t - B + 3) + 1)
            turn_x(6)
            turn_x(7)

            def project_qk(h, j):
                p = (j + 1) % 2
                for k, (w_hi, w_lo, x_hi, x_lo) in enumerate(((wk_hi, wk_lo, ctxT_hi, ctxT_lo),
                                                              (wq_hi, wq_lo, xT_hi, xT_lo))):
                    pe.wait_ge(lo_made, split_k(h) + k)
                    for half in range(2):
                        if k == 1:
                            pe.wait_ge(qk_copied, 4 * h + half + 1)
                            if is_first(h):
                                pe.wait_ge(x_lo_made, HALF * (half + 1))
                        elif is_first(h):
                            pe.wait_ge(v_copied, B - 1 + half)
                        elif p == 1 and not (isinstance(h, int) and h == 1):
                            pe.wait_ge(out_added, 4 * (h - 3) + B - 1 + half)
                        else:
                            pe.wait_ge(qk_copied, 4 * (h - 1) + 3 + half)
                        at = slice(half * BANK, (half + 1) * BANK)
                        product(proj[half][:, :], chunks(w_hi[:, p, :, :], w_lo[:, p, :, :]),
                                chunks(x_hi[:, :, at], x_lo[:, :, at])).then_inc(qk_projected, 1)

            def make_scores(h):
                for half in range(2):
                    pe.wait_ge(qk_copied, 4 * h + 3 + half)
                    if not is_first(h):
                        pe.wait_ge(scores_biased, 2 * (h - 1) + half + 1)
                    for b in range(HALF * half, HALF * (half + 1)):
                        at = slice(b * P, (b + 1) * P)
                        ins = pe.matmul(score[half][:, (b % HALF) * P:(b % HALF + 1) * P], qT[:, at], kT[:, at],
                                        start=True, stop=True)
                    ins.then_inc(scores_made, 1)

            def turn_probs(h):
                for half in range(2):
                    pe.wait_ge(probs_scaled, 2 * h + half + 1)
                    if is_first(h):
                        pe.wait_ge(x_lo_made, B)
                    else:
                        pe.wait_ge(probsT_copied, 2 * (h - 1) + half + 1)
                    for b in range(HALF * half, HALF * (half + 1)):
                        ins = pe.transpose(turned[half][:, (b % HALF) * P:(b % HALF + 1) * P], probs[:, b, :],
                                           ident[:, :])
                    ins.then_inc(probs_turned, 1)

            def attend(h, j):
                for half in range(2):
                    pe.wait_ge(probsT_copied, 2 * h + half + 1)
                    if j == 0:
                        pe.wait_ge(v_copied, 2 * h + HALF * (half + 1))
                    if not is_first(h):
                        pe.wait_ge(attn_lo_made, 2 * (h - 1) + half + 1)
                    for b in range(HALF * half, HALF * (half + 1)):
                        ins = pe.matmul(attended[half][:, (b % HALF) * P:(b % HALF + 1) * P],
                                        v[:, b, j * P:(j + 1) * P], probsT[:, b, :], start=True, stop=True)
                    ins.then_inc(attn_made, 1)

            def project_out(h, j):
                pe.wait_ge(lo_made, split_before(h) + 1)
                for t in range(B):
                    if t >= 2:
                        pe.wait_ge(out_added, 4 * (h - 1) + t - 1)
                    elif j == GH - 1:
                        pe.wait_ge(v_copied, 2 * (h + 1) + B - 1 + t)
                    else:
                        pe.wait_ge(qk_copied, 4 * (h + 1) + 3 + t)
                    at = slice(t * P, (t + 1) * P)
                    waits = {1: (attn_lo_made, 2 * h + t // HALF + 1)} if t % HALF == 0 else None
                    product(proj[t % 2][:, :], [(attn_hi[:, i, at], attn_lo[:, i, at]) for i in range(2)],
                            [(wo_hi[:, i, :], wo_lo[:, i, :]) for i in range(2)],
                            waits=waits).then_inc(out_projected, 1)

            def project_out_alone(h, t, bank):
                at = slice(t * P, (t + 1) * P)
                if t % HALF == 0:
                    pe.wait_ge(attn_lo_made, 2 * h + t // HALF + 1)
                product(bank[:, :], [(attn_hi[:, h % 2, at], attn_lo[:, h % 2, at])],
                        [(wo_hi[:, h % 2, :], wo_lo[:, h % 2, :])]).then_inc(out_projected, 1)

            def step(h, j):
                if is_last(h):
                    turn_probs(h)
                    attend(h, j)
                    return
                project_qk(h + 1, j)
                if isinstance(h, int) and h == LAST - 1:
                    make_scores(h + 1)
                    turn_probs(h)
                    attend(h, j)
                    pe.wait_ge(lo_made, split_before(h) + 1)
                    for t in range(B):
                        if t >= 2:
                            pe.wait_ge(out_added, 4 * h + t - 1)
                        else:
                            pe.wait_ge(qk_copied, 4 * (h + 1) + 3 + t)
                        project_out_alone(h, t, proj[t % 2])
                    return
                turn_probs(h)
                make_scores(h + 1)
                attend(h, j)
                if j == GH - 1:
                    pe.wait_ge(lo_made, split_before(h) + 2)
                    for t in range(B):
                        if t < 2:
                            pe.wait_ge(qk_copied, 4 * (h + 1) + 3 + t)
                        else:
                            pe.wait_ge(v_copied, 2 * (h + 1) + t - 1)
                        project_v(t)
                if j % 2 == 1:
                    project_out(h, j)

            project_qk(0, GH - 1)
            make_scores(0)
            run_steps(pe, step)

            def last_out(t):
                if t >= 2:
                    pe.wait_ge(x1_made, t - 1)
                else:
                    pe.wait_ge(scores_biased, 2 * LAST + t + 1)
                project_out_alone(LAST, t, score[t % 2])

            def turn_y(t):
                pe.wait_ge(y_made, t + 1)
                if t >= 2:
                    pe.wait_ge(y_lo_made, t - 1)
                else:
                    pe.wait_ge(attn_lo_made, 2 * LAST + t + 1)
                for c in range(C):
                    ins = pe.transpose(attended[t % 2][:, c * P:(c + 1) * P], y_norm[t][:, c * P:(c + 1) * P],
                                       ident[:, :])
                ins.then_inc(y_turned, 1)

            def turned_y(t):
                at = slice((t % 2) * P, (t % 2 + 1) * P)
                return chunks(xT_hi[:, :, at], xT_lo[:, :, at])

            def project_ag(t):
                pe.wait_ge(y_lo_made, t + 1)
                if t >= 2:
                    pe.wait_ge(hw_lo_made, t - 1)
                else:
                    pe.wait_ge(probsT_copied, 2 * LAST + t + 1)
                product(turned[t % 2][:, 0:AG], turned_y(t), chunks(ag_hi, ag_lo)).then_inc(ag_projected, 1)

            def project_base(t):
                if t >= 2:
                    pe.wait_ge(out_made, t - 1)
                else:
                    pe.wait_ge(out_added, 4 * H - 1 + t)
                product(proj[t % 2][:, :], turned_y(t), chunks(wv_hi, wv_lo), stop=False).then_inc(base_projected, 1)

            def turn_hw(t):
                pe.wait_ge(hw_made, t + 1)
                pe.transpose(turned[t % 2][:, 2 * P:3 * P], hw[:, t % 2, :], ident[:, :]).then_inc(hw_turned, 1)

            def add_delta(t):
                pe.wait_ge(hw_lo_made, t + 1)
                product(proj[t % 2][:, :], [(hwT_hi[:, t % 2, :], hwT_lo[:, t % 2, :])], [(wb_hi, wb_lo)],
                        start=False).then_inc(delta_added, 1)

            pe.wait_ge(lo_made, split_before(H))
            for t in range(3):
                last_out(t)
            turn_y(0)
            for t in range(B + 1):
                if t + 3 < B:
                    last_out(t + 3)
                if t + 1 < B:
                    turn_y(t + 1)
                if t < B:
                    project_ag(t)
                if t >= 1:
                    turn_hw(t - 1)
                if t < B:
                    project_base(t)
                if t >= 1:
                    add_delta(t - 1)


def kernel(x, ctx_4096, mask_BxSxS2_bk0, g_xattn, g_ffn, L0_xattn_position_bias, L0_xattn_ln_weight, L0_xattn_w_q,
           L0_xattn_w_k, L0_xattn_w_v, L0_xattn_w_out, L0_ffn_W_base, L0_ffn_b_base, L0_ffn_W_gate, L0_ffn_A,
           L0_ffn_B):
    import numpy as np
    import concourse.bacc as bacc
    from concourse.bass_utils import run_bass_kernel_spmd

    def by_head(w):
        return np.asarray(w).reshape(H, P, C, P).transpose(0, 3, 2, 1).reshape(H, P, D)

    ag = np.concatenate([np.asarray(L0_ffn_A).reshape(ER, D), np.asarray(L0_ffn_W_gate)], axis=0)
    laid = {
        "x": x,
        "ctx": np.asarray(ctx_4096).reshape(B, P, C, P).transpose(3, 0, 2, 1).reshape(P, B, D),
        "mask": np.asarray(mask_BxSxS2_bk0).transpose(1, 0, 2),
        "gates": np.concatenate([np.asarray(g_xattn), np.asarray(g_ffn)]),
        "bias": L0_xattn_position_bias,
        "ln_w": np.asarray(L0_xattn_ln_weight).reshape(C, P).T,
        "w_q": by_head(L0_xattn_w_q),
        "w_k": by_head(L0_xattn_w_k),
        "w_v": np.asarray(L0_xattn_w_v).reshape(G, GH * P, C, P).transpose(0, 2, 3, 1).reshape(G * C, P, GH * P),
        "w_o": np.asarray(L0_xattn_w_out).T.reshape(H, P, D),
        "w_base": np.asarray(L0_ffn_W_base).T.reshape(C, P, D),
        "b_base": L0_ffn_b_base,
        "w_ag": ag.reshape(AG, C, P).transpose(2, 1, 0).reshape(P, C * AG),
        "w_b": np.asarray(L0_ffn_B).transpose(0, 2, 1).reshape(ER, D),
    }
    nc = bacc.Bacc("TRN2", target_bir_lowering=False, num_devices=1)
    arrays, args = {}, []
    for name, a in laid.items():
        a = np.ascontiguousarray(a)
        arrays[f"in_{name}"] = a
        args.append(nc.dram_tensor(f"in_{name}", a.shape, mybir.dt.from_np(a.dtype), kind="ExternalInput").ap())
    args.append(nc.dram_tensor("out_dram", (B, P, D), F32, kind="ExternalOutput").ap())
    program(nc, *args)
    r = run_bass_kernel_spmd(nc, [arrays], core_ids=[0])
    return r.results[0]["out_dram"]
```

```python
from contextlib import ExitStack

import concourse.bass as bass
from concourse import mybir

ALU = mybir.AluOpType
ACT = mybir.ActivationFunctionType
F32 = mybir.dt.float32
F32R = mybir.dt.float32r
U8 = mybir.dt.uint8
U32 = mybir.dt.uint32
AX_X = mybir.AxisListType.X

P = 128
B = 8
D = 512
C = D // P
H = 32
GH = 4
G = H // GH
T = B * P
HALF = B // 2
E = 8
R = 16
ER = E * R
AG = ER + E
EPS = 1e-5
MASKED = -1e30
Q = 32
WARM_UP = 9
LAST = H - 1
BEFORE_LATE = 4 * (H - 4)
BANK = 512



def split_before(h):
    return 4 * h + 4 - (2 if isinstance(h, int) and h == H - 1 else 3 if isinstance(h, int) and h == H else 0)


def split_k(h):
    if isinstance(h, int) and h < 2:
        return 1 + 2 * h
    return split_before(h - 2) + 3


def stage_count(n, parity):
    fewer = 16 * (H - n) if isinstance(n, int) and n >= H - 2 else 0
    return 32 * n + (64 if parity == 0 else 32) - fewer


def bias_count(h, parity):
    return 8 * h + (16 if parity == 0 else 8)


def program(nc, x, ctx, mask, gates, bias, ln_w, w_q, w_k, w_v, w_o, w_base, b_base, w_ag, w_b, out):
    with ExitStack() as stack:
        def sb(name, shape, dt=F32):
            return stack.enter_context(nc.sbuf_tensor(name, shape, dt))

        def pb(name):
            return stack.enter_context(nc.psum_tensor(name, [P, BANK], F32))

        def sem(name):
            return stack.enter_context(nc.semaphore(name))

        xT_hi, xT_lo = sb("xT_hi", [P, C, T], F32R), sb("xT_lo", [P, C, T], F32R)
        ctxT_hi, ctxT_lo = sb("ctxT_hi", [P, C, T], F32R), sb("ctxT_lo", [P, C, T], F32R)
        acc = sb("acc", [P, B, D])
        wq_hi, wq_lo = sb("wq_hi", [P, 2, C, P], F32R), sb("wq_lo", [P, 2, C, P], F32R)
        wk_hi, wk_lo = sb("wk_hi", [P, 2, C, P], F32R), sb("wk_lo", [P, 2, C, P], F32R)
        wv_hi, wv_lo = sb("wv_hi", [P, C, GH * P], F32R), sb("wv_lo", [P, C, GH * P], F32R)
        wo_hi, wo_lo = sb("wo_hi", [P, 2, D], F32R), sb("wo_lo", [P, 2, D], F32R)
        ag = sb("ag", [P, C, AG])
        stage = sb("stage", [P, 2, 4, D])
        qT, kT = sb("qT", [P, T]), sb("kT", [P, T])
        v = sb("v", [P, B, GH * P])
        probs, probsT = sb("probs", [P, B, P]), sb("probsT", [P, B, P])
        attn_hi, attn_lo = sb("attn_hi", [P, 2, T], F32R), sb("attn_lo", [P, 2, T], F32R)
        pos_bias = sb("pos_bias", [P, 2, P])
        mask8 = sb("mask8", [P, B, P], U8)
        mask_bias, full_bias = sb("mask_bias", [P, B, P]), sb("full_bias", [P, B, P])
        row_any, row_scale = sb("row_any", [P, B]), sb("row_scale", [P, B])
        neg_max, sums, sums_inv, prob_scale = (sb(n, [P, B]) for n in ("neg_max", "sums", "sums_inv", "prob_scale"))
        ident = sb("ident", [P, P])
        ln_w_sb = sb("ln_w_sb", [P, C])
        gates_sb, gates_tanh = sb("gates_sb", [P, 2]), sb("gates_tanh", [P, 2])
        b_base_sb = sb("b_base_sb", [P, D])
        x_factor, x_shift = sb("x_factor", [P, B]), sb("x_shift", [P, B])
        y_shift = sb("y_shift", [P, B])
        half_neg, minus_one = sb("half_neg", [P, B]), sb("minus_one", [P, 1])
        experts = sb("experts", [P, E])
        stats, moments = sb("stats", [P, B, 6]), sb("moments", [P, B, 2])
        var_eps, rstd, rms_in, rms_inv, x_scale = (
            sb(n, [P, B]) for n in ("var_eps", "rstd", "rms_in", "rms_inv", "x_scale"))
        logits, top8, top_i = sb("logits", [P, 2, E]), sb("top8", [P, 2, 8]), sb("top_i", [P, 2, 8], U32)
        top_f = sb("top_f", [P, 2, 2])
        gap, ratio, ratio1, w_first, w_second = (
            sb(n, [P, 2]) for n in ("gap", "ratio", "ratio1", "w_first", "w_second"))
        route1, route2, route = (sb(n, [P, 2, E]) for n in ("route1", "route2", "route"))
        hw = sb("hw", [P, 2, ER])
        hwT_hi, hwT_lo = sb("hwT_hi", [P, 2, P], F32R), sb("hwT_lo", [P, 2, P], F32R)

        y_norm = [stage[:, t // HALF, t % HALF, :] for t in range(B)]
        wb_hi = wq_hi[:, 0, :, :].rearrange("p c n -> p (c n)")
        wb_lo = wq_lo[:, 0, :, :].rearrange("p c n -> p (c n)")
        y_whole = [qT[:, i * BANK:(i + 1) * BANK] for i in range(2)]
        x_norm = [buf[:, HALF * i:HALF * (i + 1), :] for buf in (full_bias, probs, probsT) for i in range(2)]
        x_norm += [qT[:, i * BANK:(i + 1) * BANK].rearrange("p (c n) -> p c n", c=C) for i in range(2)]
        ctx_raw = [v[:, b, :].rearrange("p (c t) -> p c t", c=C) for b in range(B)]

        proj = [pb("proj0"), pb("proj1")]
        score = [pb("score0"), pb("score1")]
        turned = [pb("turned0"), pb("turned1")]
        attended = [pb("attended0"), pb("attended1")]
        x_bank = turned + attended

        stage_loaded = [sem("stage_loaded0"), sem("stage_loaded1")]
        bias_loaded = [sem("bias_loaded0"), sem("bias_loaded1")]
        first_v_loaded = [sem(f"first_v_loaded{c}") for c in range(C)]
        first_qk_loaded = [sem(f"first_qk_loaded{i}") for i in range(4)]
        ctx_loaded = [sem(f"ctx_loaded{b}") for b in range(B)]
        x_loaded = [sem("x_loaded0"), sem("x_loaded1")]
        small_loaded = sem("small_loaded")
        ag_loaded = sem("ag_loaded")
        out_stored = sem("out_stored")
        hi_made, lo_made = sem("hi_made"), sem("lo_made")
        ident_made, consts_made, mask_made, x_scale_made = (
            sem(n) for n in ("ident_made", "consts_made", "mask_made", "x_scale_made"))
        first_v_hi_made, first_v_lo_made = sem("first_v_hi_made"), sem("first_v_lo_made")
        ctx_hi_made, ctx_lo_made = sem("ctx_hi_made"), sem("ctx_lo_made")
        ln_chain, ln_pow = sem("ln_chain"), sem("ln_pow")
        x_normed, x_turned, x_hi_made, x_lo_made = (
            sem(n) for n in ("x_normed", "x_turned", "x_hi_made", "x_lo_made"))
        h_made, tanh_made = sem("h_made"), sem("tanh_made")
        bias_scaled = sem("bias_scaled")
        qk_projected, qk_copied = sem("qk_projected"), sem("qk_copied")
        v_projected, v_copied = sem("v_projected"), sem("v_copied")
        bias_made = sem("bias_made")
        scores_made, scores_biased, max_made = sem("scores_made"), sem("scores_biased"), sem("max_made")
        exp_made, sums_inverted, scale_made = sem("exp_made"), sem("sums_inverted"), sem("scale_made")
        probs_scaled, probs_turned, probsT_copied = (
            sem(n) for n in ("probs_scaled", "probs_turned", "probsT_copied"))
        attn_made, attn_hi_made, attn_lo_made = sem("attn_made"), sem("attn_hi_made"), sem("attn_lo_made")
        out_projected, out_added = sem("out_projected"), sem("out_added")
        x1_made, f_chain, f_var, f_pow = sem("x1_made"), sem("f_chain"), sem("f_var"), sem("f_pow")
        y_made, y_turned, y_copied, y_hi_made, y_lo_made = (
            sem(n) for n in ("y_made", "y_turned", "y_copied", "y_hi_made", "y_lo_made"))
        ag_projected = sem("ag_projected")
        experts_found, route_chain, route_made = sem("experts_found"), sem("route_chain"), sem("route_made")
        gap_made, ratio_made, hw_made, hw_turned = (
            sem(n) for n in ("gap_made", "ratio_made", "hw_made", "hw_turned"))
        hw_hi_made, hw_lo_made, delta_added = sem("hw_hi_made"), sem("hw_lo_made"), sem("delta_added")
        x1_shifted, out_made = sem("x1_shifted"), sem("out_made")

        def run_steps(eng, step):
            for h in range(GH):
                step(h, h % GH)
            with eng.Fori(1, G - 1) as g:
                for j in range(GH):
                    step(g * GH + j, j)
            for h in range(H - GH, H):
                step(h, h % GH)

        def turned_by_pe(h):
            return isinstance(h, int) and h in (0, LAST)

        def is_last(h):
            return isinstance(h, int) and h == LAST

        def is_first(h):
            return isinstance(h, int) and h == 0

        def in_last_pair(h):
            return isinstance(h, int) and h >= H - 2

        def wo_place(h, p):
            if in_last_pair(h):
                return tuple(w[:, p, :, :].rearrange("p c n -> p (c n)") for w in (wk_hi, wk_lo))
            return wo_hi[:, p, :], wo_lo[:, p, :]

        def attn_place(h, p):
            if in_last_pair(h):
                return ctxT_hi[:, p, :], ctxT_lo[:, p, :]
            return attn_hi[:, p, :], attn_lo[:, p, :]

        def pieces(h, j):
            raw = [stage[:, j % 2, i, :] for i in range(4)]
            four = [r.rearrange("p (c n) -> p c n", c=C) for r in raw]
            p = j % 2
            found = [wo_place(h, p) + (raw[0],), (wv_hi[:, j, :], wv_lo[:, j, :], raw[1])]
            if not isinstance(h, int) or h + 2 <= LAST:
                found += [(wk_hi[:, p, :, :], wk_lo[:, p, :, :], four[2]),
                          (wq_hi[:, p, :, :], wq_lo[:, p, :, :], four[3])]
            elif h == LAST:
                found.append((wb_hi, wb_lo, raw[2]))
            return found

        first_v = [(wv_hi[:, c, :], wv_lo[:, c, :], stage[:, 1, c, :]) for c in range(C)]
        first_qk = []
        for i in range(2):
            for k, (hi, lo) in enumerate(((wk_hi, wk_lo), (wq_hi, wq_lo))):
                raw = stage[:, 0, 2 * i + k, :].rearrange("p (c n) -> p c n", c=C)
                first_qk.append((hi[:, i, :, :], lo[:, i, :, :], raw))

        def ag_bank(t):
            return score[0] if t == B - 1 else turned[t % 2]

        def base_bank(t):
            return score[1] if t == B - 1 else proj[t % 2]

        block = stack.enter_context(nc.Block())

        @block.sync
        def _(sp):
            def load_first(c, tiles):
                sp.dma_start(stage[:, 1, c, :], w_v[c, :, :]).then_inc(first_v_loaded[c], 16)
                for b in tiles:
                    sp.dma_start(v[:, b, :], ctx[:, b, :]).then_inc(ctx_loaded[b], 16)

            load_first(0, [0])
            load_first(1, [])
            load_first(2, [])
            load_first(3, [1, 2, 3])
            sp.dma_start(mask8[:, :, :], mask).then_inc(small_loaded, 16)
            sp.dma_start(ln_w_sb[:, :], ln_w).then_inc(small_loaded, 16)
            sp.dma_start(gates_sb[:, :], gates.partition_broadcast(P)).then_inc(small_loaded, 16)
            sp.dma_start(b_base_sb[:, :], b_base.partition_broadcast(P)).then_inc(small_loaded, 16)

            def load_x(i):
                sp.dma_start(acc[:, HALF * i:HALF * (i + 1), :],
                             x[HALF * i:HALF * (i + 1), :, :].rearrange("b p d -> p b d")).then_inc(x_loaded[i], 16)

            load_x(0)
            for b in range(4, B):
                sp.dma_start(v[:, b, :], ctx[:, b, :]).then_inc(ctx_loaded[b], 16)
            for i in range(2):
                sp.dma_start(stage[:, 0, 2 * i, :], w_k[i, :, :]).then_inc(first_qk_loaded[2 * i], 16)
                sp.dma_start(stage[:, 0, 2 * i + 1, :], w_q[i, :, :]).then_inc(first_qk_loaded[2 * i + 1], 16)
                if i == 0:
                    load_x(1)
            for i in range(2):
                sp.dma_start(pos_bias[:, i, :], bias[i, :, :]).then_inc(bias_loaded[i], 16)

            def step(n, j):
                p = j % 2
                if isinstance(n, int) and n == 1:
                    sp.wait_ge(first_v_lo_made, C)
                else:
                    sp.wait_ge(lo_made, 4 if isinstance(n, int) and n == 0 else split_before(n - 1))
                sp.dma_start(stage[:, p, 0, :], w_o[n, :, :]).then_inc(stage_loaded[p], 16)
                wide = w_base[j, :, :] if isinstance(n, int) and n >= H - GH else w_v[n + GH, :, :]
                sp.dma_start(stage[:, p, 1, :], wide).then_inc(stage_loaded[p], 16)
                if not isinstance(n, int) or n + 2 <= LAST:
                    sp.dma_start(stage[:, p, 2, :], w_k[n + 2, :, :]).then_inc(stage_loaded[p], 16)
                    sp.dma_start(stage[:, p, 3, :], w_q[n + 2, :, :]).then_inc(stage_loaded[p], 16)
                elif n == LAST:
                    sp.dma_start(ag[:, :, :], w_ag.rearrange("p (c n) -> p c n", c=C)).then_inc(ag_loaded, 16)
                    sp.dma_start(stage[:, p, 2, :], w_b).then_inc(stage_loaded[p], 16)
                if not isinstance(n, int) or n + 2 <= LAST:
                    sp.wait_ge(bias_made, n + 1)
                    sp.dma_start(pos_bias[:, p, :], bias[n + 2, :, :]).then_inc(bias_loaded[p], 16)

            run_steps(sp, step)

            for t in range(B):
                sp.wait_ge(out_made, t + 1)
                sp.dma_start(out[t, :, :], acc[:, t, :]).then_inc(out_stored, 16)
            sp.wait_ge(out_stored, 16 * B)

        @block.gpsimd
        def _(pool):
            pool.memset(ident[:, :], 0.0).then_inc(ident_made, 1)
            pool.memset(half_neg[:, :], -0.5).then_inc(consts_made, 1)
            pool.memset(minus_one[:, :], -1.0).then_inc(consts_made, 1)
            for e in range(E):
                pool.memset(experts[:, e:e + 1], float(e)).then_inc(consts_made, 1)
            pool.wait_ge(ident_made, 1)
            pool.affine_select(out=ident[:, :], in_=ident[:, :], compare_op=ALU.not_equal, fill=1.0,
                               base=0, pattern=[[-1, P]], channel_multiplier=1).then_inc(ident_made, 1)
            pool.wait_ge(consts_made, 2 + E)

            def make_lo(piece, n):
                hi, lo, raw = piece
                pool.wait_ge(hi_made, n)
                pool.tensor_tensor(lo, raw, hi.bitcast(F32), ALU.subtract).then_inc(lo_made, 1)

            for half in range(2):
                a, b = HALF * half, HALF * (half + 1)
                pool.wait_ge(ln_chain, 4 * half + 1)
                pool.tensor_tensor(rstd[:, a:b], var_eps[:, a:b], half_neg[:, a:b], ALU.pow).then_inc(ln_pow, 1)
                pool.wait_ge(ln_chain, 4 * half + 4)
                pool.tensor_tensor(rms_inv[:, a:b], rms_in[:, a:b], half_neg[:, a:b], ALU.pow).then_inc(ln_pow, 1)
                for i in range(2 * half, 2 * half + 2):
                    make_lo(first_qk[i], 1 + i)

            def add_bias(h, j):
                p = j % 2
                pool.wait_ge(bias_loaded[p], bias_count(h, p))
                if is_first(h):
                    pool.wait_ge(mask_made, 1)
                    pool.wait_ge(x_turned, 2)
                else:
                    pool.wait_ge(scores_biased, 2 * h)
                pool.tensor_tensor(full_bias[:, :, :], mask_bias[:, :, :],
                                   pos_bias[:, p, :].unsqueeze(1).broadcast_to([P, B, P]),
                                   ALU.add).then_inc(bias_made, 1)

            add_bias(0, 0)

            def scale_probs(h):
                for half in range(2):
                    a, b = HALF * half, HALF * (half + 1)
                    pool.wait_ge(scale_made, 2 * h + half + 1)
                    pool.tensor_tensor(probs[:, a:b, :], probs[:, a:b, :],
                                       prob_scale[:, a:b].unsqueeze(2).broadcast_to([P, HALF, P]),
                                       ALU.mult).then_inc(probs_scaled, 1)

            def step(h, j):
                for i, piece in enumerate(pieces(h, j)):
                    make_lo(piece, split_before(h) + 1 + i)
                if not is_last(h):
                    scale_probs(h + 1)
                if not isinstance(h, int) or h + 2 <= LAST:
                    add_bias(h + 2, j)

            scale_probs(0)
            add_bias(1, 1)
            run_steps(pool, step)

            pool.wait_ge(tanh_made, 1)
            pool.tensor_scalar(b_base_sb[:, :], b_base_sb[:, :], gates_tanh[:, 1:2], None, ALU.mult).then_inc(bias_scaled, 1)
            pool.wait_ge(bias_scaled, 1)

            def weigh_experts(t):
                p = t % 2
                one = slice(p, p + 1)
                pool.wait_ge(ratio_made, t + 1)
                pool.tensor_scalar(ratio1[:, one], ratio[:, one], 1.0, None, ALU.add).then_inc(route_chain, 1)
                pool.wait_ge(route_chain, 4 * t + 1)
                pool.tensor_tensor(w_first[:, one], ratio1[:, one], minus_one[:, 0:1], ALU.pow).then_inc(route_chain, 1)
                pool.wait_ge(route_chain, 4 * t + 2)
                pool.tensor_tensor(w_second[:, one], ratio[:, one], w_first[:, one], ALU.mult).then_inc(route_chain, 1)
                pool.wait_ge(experts_found, t + 1)
                if t >= 2:
                    pool.wait_ge(hw_made, t - 1)
                pool.wait_ge(route_chain, 4 * t + 3)
                pool.tensor_scalar(route1[:, p, :], experts[:, :], top_f[:, p, 0:1], w_first[:, one],
                                   ALU.is_equal, ALU.mult)
                pool.tensor_scalar(route2[:, p, :], experts[:, :], top_f[:, p, 1:2], w_second[:, one],
                                   ALU.is_equal, ALU.mult).then_inc(route_chain, 1)
                pool.wait_ge(route_chain, 4 * t + 4)
                pool.tensor_tensor(route[:, p, :], route1[:, p, :], route2[:, p, :], ALU.add).then_inc(route_made, 1)

            for t in range(-3, B):
                if t + 3 < B:
                    u = t + 3
                    one = slice(u, u + 1)
                    pool.wait_ge(f_var, u + 1)
                    pool.tensor_tensor(rstd[:, one], var_eps[:, one], half_neg[:, one], ALU.pow).then_inc(f_pow, 1)
                    pool.wait_ge(f_pow, 2 * u + 1)
                    pool.tensor_scalar(y_shift[:, one], moments[:, u, 0:1], rstd[:, one], -1.0,
                                       ALU.mult, ALU.mult).then_inc(f_pow, 1)
                if 0 <= t < B - 1:
                    weigh_experts(t)
                if t == B - 2:
                    weigh_experts(B - 1)
                if t >= 0:
                    pool.wait_ge(y_made, t + 1)
                    pool.tensor_tensor(acc[:, t, :], acc[:, t, :], b_base_sb[:, :], ALU.add).then_inc(x1_shifted, 1)

        @block.scalar
        def _(act):
            def make_hi(piece):
                hi, _, raw = piece
                act.activation(hi, raw, ACT.Copy).then_inc(hi_made, 1)

            def copy_v(t):
                act.wait_ge(v_projected, t + 1)
                act.activation(v[:, t, :], proj[t % 2][:, :], ACT.Copy).then_inc(v_copied, 1)

            def copy_v_next(h, t):
                act.wait_ge(v_projected, 2 * (h + 1) + t + 1)
                act.wait_ge(attn_made, 2 * h + t // HALF + 1)
                act.activation(v[:, t, :], proj[t % 2][:, :], ACT.Copy).then_inc(v_copied, 1)

            def first_v_hi(c):
                act.wait_ge(first_v_loaded[c], 16)
                act.activation(first_v[c][0], first_v[c][2], ACT.Copy).then_inc(first_v_hi_made, 1)

            def ctx_hi(b):
                act.wait_ge(ctx_loaded[b], 16)
                act.activation(ctxT_hi[:, :, b * P:(b + 1) * P], ctx_raw[b], ACT.Copy).then_inc(ctx_hi_made, 1)

            def x_hi(b):
                act.wait_ge(x_turned, b + 1)
                for c in range(C):
                    ins = act.activation(xT_hi[:, c, b * P:(b + 1) * P], x_bank[b % 4][:, c * P:(c + 1) * P],
                                         ACT.Identity, scale=ln_w_sb[:, c:c + 1])
                ins.then_inc(x_hi_made, 1)

            def copy_kq(h, k, half):
                act.wait_ge(qk_projected, 4 * h + 2 * k + half + 1)
                if not is_first(h):
                    act.wait_ge(scores_made, 2 * (h - 1) + half + 1)
                act.activation((kT, qT)[k][:, half * BANK:(half + 1) * BANK], proj[half][:, :],
                               ACT.Copy).then_inc(qk_copied, 1)

            first_v_hi(0)
            ctx_hi(0)
            for c in range(1, C):
                first_v_hi(c)
            def first_qk_hi(i):
                act.wait_ge(first_qk_loaded[i], 16)
                make_hi(first_qk[i])

            for b in range(1, HALF):
                ctx_hi(b)
            act.wait_ge(small_loaded, 16 * 4)
            act.activation(gates_tanh[:, :], gates_sb[:, :], ACT.Tanh).then_inc(tanh_made, 1)
            copy_v(0)
            copy_v(1)
            ctx_hi(4)
            ctx_hi(5)
            copy_v(2)
            ctx_hi(6)
            ctx_hi(7)
            first_qk_hi(0)
            first_qk_hi(1)
            copy_v(3)
            copy_v(4)
            for b in range(3):
                x_hi(b)
            copy_v(5)
            x_hi(3)
            first_qk_hi(2)
            first_qk_hi(3)
            copy_v(6)
            copy_v(7)
            for half in range(2):
                for b in range(HALF + 2 * half, HALF + 2 * half + 2):
                    x_hi(b)
                copy_kq(0, 0, half)

            def exp_scores(h, half):
                act.wait_ge(max_made, 2 * h + half + 1)
                for b in range(HALF * half, HALF * (half + 1)):
                    ins = act.activation(probs[:, b, :], probs[:, b, :], ACT.Exp, bias=neg_max[:, b:b + 1],
                                         scale=1.0, accum_out=sums[:, b:b + 1])
                ins.then_inc(exp_made, 1)

            def step(h, j):
                found = pieces(h, j)
                if not is_last(h):
                    copy_kq(h + 1, 0, 0)
                act.wait_ge(stage_loaded[j % 2], stage_count(h, j % 2))
                if j % 2 == 0 and not is_first(h) and not in_last_pair(h):
                    act.wait_ge(out_projected, 4 * h)
                make_hi(found[0])
                if j == 0:
                    act.wait_ge(v_projected, 2 * h + B)
                make_hi(found[1])
                if not is_last(h):
                    copy_kq(h + 1, 0, 1)
                for piece in found[2:]:
                    make_hi(piece)
                if not is_last(h):
                    copy_kq(h + 1, 1, 0)
                    copy_kq(h + 1, 1, 1)
                for half in range(2 if turned_by_pe(h) else 0):
                    act.wait_ge(probs_turned, 2 * h + half + 1)
                    if not is_first(h):
                        act.wait_ge(attn_made, 2 * (h - 1) + half + 1)
                    act.activation(probsT[:, HALF * half:HALF * (half + 1), :], turned[half][:, :],
                                   ACT.Copy).then_inc(probsT_copied, 1)
                for half in range(2):
                    act.wait_ge(attn_made, 2 * h + half + 1)
                    if j % 2 == 0 and half == 0 and not is_first(h) and not in_last_pair(h):
                        act.wait_ge(out_projected, 4 * h)
                    act.activation(attn_place(h, j % 2)[0][:, half * BANK:(half + 1) * BANK], attended[half][:, :],
                                   ACT.Copy).then_inc(attn_hi_made, 1)
                    if not is_last(h):
                        exp_scores(h + 1, half)
                if j == GH - 1 and not is_last(h):
                    for t in range(B):
                        copy_v_next(h, t)

            copy_kq(0, 1, 0)
            copy_kq(0, 1, 1)
            exp_scores(0, 0)
            exp_scores(0, 1)
            run_steps(act, step)

            def make_y(t):
                act.wait_ge(f_pow, 2 * t + 2)
                act.activation(y_norm[t], acc[:, t, :], ACT.Identity, bias=y_shift[:, t:t + 1],
                               scale=rstd[:, t:t + 1]).then_inc(y_made, 1)

            def y_hi(t):
                act.wait_ge(y_turned, t + 1)
                if t >= 2:
                    act.wait_ge(ag_projected, t - 1)
                act.activation(y_whole[t % 2], attended[t % 2][:, :], ACT.Copy).then_inc(y_copied, 1)
                act.activation(xT_hi[:, :, t * P:(t + 1) * P],
                               attended[t % 2][:, :].rearrange("p (c t) -> p c t", c=C),
                               ACT.Copy).then_inc(y_hi_made, 1)

            def hw_hi(t):
                act.wait_ge(hw_turned, t + 1)
                if t >= 2:
                    act.wait_ge(delta_added, t - 1)
                act.activation(hwT_hi[:, t % 2, :], ag_bank(t)[:, 2 * P:3 * P], ACT.Copy).then_inc(hw_hi_made, 1)

            def find_ratio(t):
                act.wait_ge(gap_made, t + 1)
                act.activation(ratio[:, t % 2:t % 2 + 1], gap[:, t % 2:t % 2 + 1], ACT.Exp).then_inc(ratio_made, 1)

            act.wait_ge(lo_made, split_before(H))
            make_y(0)
            make_y(1)
            y_hi(0)
            for t in range(B + 1):
                if t + 1 < B:
                    y_hi(t + 1)
                if t >= 1:
                    hw_hi(t - 1)
                if t < B - 1:
                    find_ratio(t)
                if t == B - 2:
                    find_ratio(B - 1)
                if t + 2 < B:
                    make_y(t + 2)

        @block.vector
        def _(dve):
            def first_v_lo(c):
                hi, lo, raw = first_v[c]
                dve.wait_ge(first_v_hi_made, c + 1)
                dve.tensor_tensor(lo, raw, hi.bitcast(F32), ALU.subtract).then_inc(first_v_lo_made, 1)

            def ctx_lo(b):
                dve.wait_ge(ctx_hi_made, b + 1)
                at = slice(b * P, (b + 1) * P)
                dve.tensor_tensor(ctxT_lo[:, :, at], ctx_raw[b], ctxT_hi[:, :, at].bitcast(F32),
                                  ALU.subtract).then_inc(ctx_lo_made, 1)

            def norm_x(half, meanwhile):
                a, b = HALF * half, HALF * (half + 1)
                dve.wait_ge(x_loaded[half], 16)
                for t in range(a, b):
                    dve.bn_stats(stats[:, t, :], acc[:, t, :]).then_inc(f_chain, 1)
                dve.wait_ge(f_chain, 2 * b - HALF)
                for t in range(a, b):
                    dve.bn_aggr(moments[:, t, :], stats[:, t, :]).then_inc(f_chain, 1)
                dve.wait_ge(f_chain, 2 * b)
                mean, var = moments[:, a:b, 0], moments[:, a:b, 1]
                dve.tensor_scalar(var_eps[:, a:b], var, EPS, None, ALU.add).then_inc(ln_chain, 1)
                meanwhile[0]()
                dve.wait_ge(ln_pow, 2 * half + 1)
                dve.tensor_tensor(rms_in[:, a:b], var, rstd[:, a:b], ALU.mult).then_inc(ln_chain, 1)
                dve.wait_ge(ln_chain, 4 * half + 2)
                dve.tensor_tensor(rms_in[:, a:b], rms_in[:, a:b], rstd[:, a:b], ALU.mult).then_inc(ln_chain, 1)
                dve.wait_ge(ln_chain, 4 * half + 3)
                dve.tensor_scalar(rms_in[:, a:b], rms_in[:, a:b], EPS, None, ALU.add).then_inc(ln_chain, 1)
                meanwhile[1]()
                dve.wait_ge(ln_pow, 2 * half + 2)
                dve.tensor_tensor(x_scale[:, a:b], rstd[:, a:b], rms_inv[:, a:b], ALU.mult).then_inc(x_scale_made, 1)
                dve.wait_ge(x_scale_made, half + 1)
                for t in range(a, b):
                    dve.tensor_scalar(x_norm[t], acc[:, t, :].rearrange("p (c n) -> p c n", c=C),
                                      moments[:, t, 0:1], x_scale[:, t:t + 1],
                                      ALU.subtract, ALU.mult).then_inc(x_normed, 1)

            def begin_sums():
                dve.wait_ge(x_normed, B)
                dve.tensor_scalar(x_factor[:, :], rstd[:, :], gates_tanh[:, 0:1], None, ALU.mult).then_inc(h_made, 1)
                dve.wait_ge(h_made, 1)
                dve.tensor_tensor(x_shift[:, :], moments[:, :, 0], x_factor[:, :], ALU.mult).then_inc(h_made, 1)
                dve.wait_ge(h_made, 2)
                dve.tensor_scalar(x_factor[:, :], x_factor[:, :], 1.0, None, ALU.add).then_inc(h_made, 1)
                dve.wait_ge(h_made, 3)
                for t in range(B):
                    dve.tensor_scalar(acc[:, t, :], acc[:, t, :], x_factor[:, t:t + 1], x_shift[:, t:t + 1],
                                      ALU.mult, ALU.subtract).then_inc(h_made, 1)

            def x_lo(t):
                dve.wait_ge(x_hi_made, t + 1)
                for c in range(C):
                    at = slice(t * P, (t + 1) * P)
                    ins = dve.scalar_tensor_tensor(out=xT_lo[:, c, at], in0=x_bank[t % 4][:, c * P:(c + 1) * P],
                                                   scalar=ln_w_sb[:, c:c + 1], in1=xT_hi[:, c, at].bitcast(F32),
                                                   op0=ALU.mult, op1=ALU.subtract)
                ins.then_inc(x_lo_made, 1)

            first_v_lo(0)
            ctx_lo(0)
            for c in range(1, C):
                first_v_lo(c)
            for b in range(1, HALF):
                ctx_lo(b)
            dve.wait_ge(small_loaded, 16 * 4)
            dve.tensor_scalar(mask_bias[:, :, :], mask8[:, :, :], -MASKED, MASKED, ALU.mult, ALU.add).then_inc(mask_made, 1)
            dve.tensor_reduce(row_any[:, :], mask8[:, :, :], AX_X, ALU.max).then_inc(mask_made, 1)
            dve.wait_ge(tanh_made, 1)
            dve.wait_ge(mask_made, 2)
            dve.tensor_scalar(row_scale[:, :], row_any[:, :], gates_tanh[:, 0:1], None, ALU.mult).then_inc(mask_made, 1)
            norm_x(0, [lambda: (ctx_lo(4), ctx_lo(5)), lambda: (ctx_lo(6), ctx_lo(7))])
            norm_x(1, [lambda: x_lo(0), lambda: x_lo(1)])
            for t in range(2, B):
                x_lo(t)

            def add_scores_bias(h, half):
                a, b = HALF * half, HALF * (half + 1)
                dve.wait_ge(scores_made, 2 * h + half + 1)
                dve.wait_ge(bias_made, h + 1)
                if not is_first(h):
                    dve.wait_ge(probs_turned, 2 * (h - 1) + half + 1)
                dve.tensor_tensor(probs[:, a:b, :], score[half][:, :].rearrange("p (b k) -> p b k", b=HALF),
                                  full_bias[:, a:b, :], ALU.add).then_inc(scores_biased, 1)

            def take_max(h, half):
                a, b = HALF * half, HALF * (half + 1)
                dve.wait_ge(scores_biased, 2 * h + half + 1)
                dve.tensor_reduce(neg_max[:, a:b], probs[:, a:b, :], AX_X, ALU.max, negate=True).then_inc(max_made, 1)

            def prob_scales(h, half):
                a, b = HALF * half, HALF * (half + 1)
                dve.wait_ge(exp_made, 2 * h + half + 1)
                dve.reciprocal(sums_inv[:, a:b], sums[:, a:b]).then_inc(sums_inverted, 1)
                dve.wait_ge(sums_inverted, 2 * h + half + 1)
                dve.tensor_tensor(prob_scale[:, a:b], sums_inv[:, a:b], row_scale[:, a:b], ALU.mult).then_inc(scale_made, 1)

            def turn_probs(h, parts):
                for part in range(parts):
                    a, b = B // parts * part, B // parts * (part + 1)
                    dve.wait_ge(probs_scaled, 2 * h + b // HALF)
                    dve.wait_ge(attn_made, 2 * (h - 1) + b // HALF)
                    for rows in range(0, P, Q):
                        for cols in range(0, P, Q):
                            ins = dve.transpose(probsT[cols:cols + Q, a:b, rows:rows + Q],
                                                probs[rows:rows + Q, a:b, cols:cols + Q])
                    ins.then_inc(probs_turned, 2 // parts)

            def attn_rest(h, j, half):
                dve.wait_ge(attn_hi_made, 2 * h + half + 1)
                at = slice(half * BANK, (half + 1) * BANK)
                hi, lo = attn_place(h, j % 2)
                dve.tensor_tensor(lo[:, at], attended[half][:, :], hi[:, at].bitcast(F32),
                                  ALU.subtract).then_inc(attn_lo_made, 1)

            def add_out(n, t):
                dve.wait_ge(out_projected, n + 1)
                dve.tensor_tensor(acc[:, t, :], proj[t % 2][:, :], acc[:, t, :], ALU.add).then_inc(out_added, 1)

            def step(h, j):
                if not is_last(h):
                    add_scores_bias(h + 1, 0)
                    take_max(h + 1, 0)
                attn_rest(h, j, 0)
                if not is_last(h):
                    add_scores_bias(h + 1, 1)
                    take_max(h + 1, 1)
                attn_rest(h, j, 1)
                if is_last(h):
                    add_out(BEFORE_LATE + B - 1, B - 1)
                    return
                n = None
                if isinstance(h, int) and h == LAST - 1:
                    n = BEFORE_LATE
                elif j % 2 == 1 and not (isinstance(h, int) and h == LAST - 2):
                    n = 4 * (h - 1)
                if n is None or j == GH - 1:
                    prob_scales(h + 1, 0)
                    prob_scales(h + 1, 1)
                    turn_probs(h + 1, 1 if j == GH - 1 else 2)
                if n is not None:
                    if isinstance(h, int) and h == 1:
                        dve.wait_ge(h_made, 3 + B)
                    else:
                        dve.wait_ge(out_added, n)
                    for t in range(B - 1 if isinstance(h, int) and h == LAST - 1 else B):
                        add_out(n + t, t)
                        if t in (1, 3) and j != GH - 1:
                            prob_scales(h + 1, t // 2)
                    if j != GH - 1 and not turned_by_pe(h + 1):
                        turn_probs(h + 1, 1)

            add_scores_bias(0, 0)
            take_max(0, 0)
            add_scores_bias(0, 1)
            take_max(0, 1)
            prob_scales(0, 0)
            prob_scales(0, 1)
            begin_sums()
            run_steps(dve, step)

            def make_x1(t):
                dve.wait_ge(out_projected, BEFORE_LATE + B + t + 1)
                if t == 0:
                    dve.wait_ge(out_added, BEFORE_LATE + B)
                dve.tensor_tensor(acc[:, t, :], score[t % 2][:, :], acc[:, t, :], ALU.add).then_inc(x1_made, 1)
                dve.wait_ge(x1_made, t + 1)
                n = 2 * B + 2 * t
                dve.bn_stats(stats[:, t, :], acc[:, t, :]).then_inc(f_chain, 1)
                dve.wait_ge(f_chain, n + 1)
                dve.bn_aggr(moments[:, t, :], stats[:, t, :]).then_inc(f_chain, 1)
                dve.wait_ge(f_chain, n + 2)
                dve.tensor_scalar(var_eps[:, t:t + 1], moments[:, t, 1:2], EPS, None, ALU.add).then_inc(f_var, 1)

            def y_lo(t):
                dve.wait_ge(y_hi_made, t + 1)
                at = slice(t * P, (t + 1) * P)
                dve.tensor_tensor(xT_lo[:, :, at], attended[t % 2][:, :].rearrange("p (c t) -> p c t", c=C),
                                  xT_hi[:, :, at].bitcast(F32), ALU.subtract).then_inc(y_lo_made, 1)

            route_steps = [0]

            def after(ins):
                route_steps[0] += 1
                ins.then_inc(ln_chain, 1)
                dve.wait_ge(ln_chain, 2 * 4 + route_steps[0])

            def find_experts(t):
                p = t % 2
                one = slice(p, p + 1)
                dve.wait_ge(ag_projected, t + 1)
                after(dve.tensor_copy(logits[:, p, :], ag_bank(t)[:, ER:AG]))
                after(dve.max(top8[:, p, :], logits[:, p, :]))
                if t >= 2:
                    dve.wait_ge(ratio_made, t - 1)
                    dve.wait_ge(route_made, t - 1)
                dve.tensor_tensor(gap[:, one], top8[:, p, 1:2], top8[:, p, 0:1], ALU.subtract).then_inc(gap_made, 1)
                after(dve.max_index(top_i[:, p, :], top8[:, p, :], logits[:, p, :]))
                dve.tensor_copy(top_f[:, p, :], top_i[:, p, 0:2]).then_inc(experts_found, 1)

            def weigh(t):
                p = t % 2
                dve.wait_ge(route_made, t + 1)
                if t >= 2:
                    dve.wait_ge(hw_turned, t - 1)
                dve.tensor_tensor(hw[:, p, :].rearrange("p (e r) -> p e r", e=E),
                                  ag_bank(t)[:, 0:ER].rearrange("p (e r) -> p e r", e=E),
                                  route[:, p, :].unsqueeze(2).broadcast_to([P, E, R]), ALU.mult).then_inc(hw_made, 1)

            def hw_lo(t):
                dve.wait_ge(hw_hi_made, t + 1)
                dve.tensor_tensor(hwT_lo[:, t % 2, :], ag_bank(t)[:, 2 * P:3 * P], hwT_hi[:, t % 2, :].bitcast(F32),
                                  ALU.subtract).then_inc(hw_lo_made, 1)

            def finish(t):
                dve.wait_ge(delta_added, t + 1)
                dve.wait_ge(x1_shifted, t + 1)
                dve.scalar_tensor_tensor(out=acc[:, t, :], in0=base_bank(t)[:, :], scalar=gates_tanh[:, 1:2],
                                         in1=acc[:, t, :], op0=ALU.mult, op1=ALU.add).then_inc(out_made, 1)

            for t in range(3):
                make_x1(t)
            y_lo(0)
            for t in range(B + 2):
                if t >= B - 1 and t <= B:
                    weigh(t - 1)
                if t == B:
                    hw_lo(B - 1)
                if t >= 2:
                    finish(t - 2)
                if 1 <= t < B - 1:
                    weigh(t - 1)
                if t + 3 < B:
                    make_x1(t + 3)
                if t + 1 < B:
                    y_lo(t + 1)
                if t < B - 1:
                    find_experts(t)
                if 1 <= t < B:
                    hw_lo(t - 1)
                if t == B - 2:
                    find_experts(B - 1)

        @block.tensor
        def _(pe):
            def product(to, left, right, start=True, stop=True, waits=None):
                n = len(left)
                waits = waits or {}
                for i, ((lh, ll), (rh, rl)) in enumerate(zip(left, right)):
                    if i in waits:
                        pe.wait_ge(*waits[i])
                    pe.matmul(to, lh, rh, start=(start and i == 0), stop=False)
                    pe.matmul(to, lh, rl, start=False, stop=False)
                    ins = pe.matmul(to, ll, rh, start=False, stop=(stop and i == n - 1))
                return ins

            def chunks(hi, lo):
                return [(hi[:, c, :], lo[:, c, :]) for c in range(C)]

            def project_v(t, waits=None):
                at = slice(t * P, (t + 1) * P)
                product(proj[t % 2][:, :], chunks(ctxT_hi[:, :, at], ctxT_lo[:, :, at]),
                        chunks(wv_hi, wv_lo), waits=waits).then_inc(v_projected, 1)

            def turn_x(t):
                pe.wait_ge(x_normed, t + 1)
                if t >= 4:
                    pe.wait_ge(x_lo_made, t - 3)
                for c in range(C):
                    ins = pe.transpose(x_bank[t % 4][:, c * P:(c + 1) * P], x_norm[t][:, c, :], ident[:, :])
                ins.then_inc(x_turned, 1)

            pe.wait_ge(ident_made, 2)
            def warm_up():
                for _ in range(WARM_UP):
                    pe.matmul(score[0][:, 0:P], ident[:, :], ident[:, :], start=True, stop=True)

            warm_up()

            for t in range(B):
                pe.wait_ge(ctx_lo_made, t + 1)
                if t >= 2:
                    pe.wait_ge(v_copied, t - 1)
                project_v(t, waits={c: (first_v_lo_made, c + 1) for c in range(C)} if t == 0 else None)
                if t == 4:
                    for i in range(HALF):
                        turn_x(i)

            operands = ((wk_hi, wk_lo, ctxT_hi, ctxT_lo), (wq_hi, wq_lo, xT_hi, xT_lo))

            def project_half(h, p, k, half):
                w_hi, w_lo, x_hi, x_lo = operands[k]
                at = slice(half * BANK, (half + 1) * BANK)
                product(proj[half][:, :], chunks(w_hi[:, p, :, :], w_lo[:, p, :, :]),
                        chunks(x_hi[:, :, at], x_lo[:, :, at])).then_inc(qk_projected, 1)

            def project_qk(h, j):
                p = (j + 1) % 2
                for k in range(2):
                    pe.wait_ge(lo_made, split_k(h) + k)
                    for half in range(2):
                        if k == 1:
                            pe.wait_ge(qk_copied, 4 * h + half + 1)
                        elif p == 1 and not (isinstance(h, int) and h in (1, LAST)):
                            pe.wait_ge(out_added, 4 * (h - 3) + B - 1 + half)
                        else:
                            pe.wait_ge(qk_copied, 4 * (h - 1) + 3 + half)
                        project_half(h, p, k, half)

            def make_scores(h, half):
                pe.wait_ge(qk_copied, 4 * h + 3 + half)
                if not is_first(h):
                    pe.wait_ge(scores_biased, 2 * (h - 1) + half + 1)
                for b in range(HALF * half, HALF * (half + 1)):
                    at = slice(b * P, (b + 1) * P)
                    ins = pe.matmul(score[half][:, (b % HALF) * P:(b % HALF + 1) * P], qT[:, at], kT[:, at],
                                    start=True, stop=True)
                ins.then_inc(scores_made, 1)

            def turn_probs(h):
                for half in range(2):
                    pe.wait_ge(probs_scaled, 2 * h + half + 1)
                    if is_first(h):
                        pe.wait_ge(x_lo_made, B)
                    for b in range(HALF * half, HALF * (half + 1)):
                        ins = pe.transpose(turned[half][:, (b % HALF) * P:(b % HALF + 1) * P], probs[:, b, :],
                                           ident[:, :])
                    ins.then_inc(probs_turned, 1)

            def attend(h, j, half):
                if turned_by_pe(h):
                    pe.wait_ge(probsT_copied, (0 if is_first(h) else 2) + half + 1)
                else:
                    pe.wait_ge(probs_turned, 2 * h + half + 1)
                if j == 0:
                    pe.wait_ge(v_copied, 2 * h + HALF * (half + 1))
                if not is_first(h):
                    pe.wait_ge(attn_lo_made, 2 * (h - 1) + half + 1)
                for b in range(HALF * half, HALF * (half + 1)):
                    ins = pe.matmul(attended[half][:, (b % HALF) * P:(b % HALF + 1) * P],
                                    v[:, b, j * P:(j + 1) * P], probsT[:, b, :], start=True, stop=True)
                ins.then_inc(attn_made, 1)

            def out_tile(h, t, bank):
                at = slice(t * P, (t + 1) * P)
                pair = [(attn_place(h - 1 + i, i), wo_place(h - 1 + i, i)) for i in range(2)]
                waits = {1: (attn_lo_made, 2 * h + t // HALF + 1)} if t % HALF == 0 else None
                product(bank[:, :], [(hi[:, at], lo[:, at]) for (hi, lo), _ in pair], [w for _, w in pair],
                        waits=waits).then_inc(out_projected, 1)

            def project_out(h, j):
                pe.wait_ge(lo_made, split_before(h) + 1)
                for t in range(B):
                    if t >= 2:
                        pe.wait_ge(out_added, 4 * (h - 1) + t - 1)
                    elif j == GH - 1:
                        pe.wait_ge(v_copied, 2 * (h + 1) + B - 1 + t)
                    else:
                        pe.wait_ge(qk_copied, 4 * (h + 1) + 3 + t)
                    out_tile(h, t, proj[t % 2])

            def project_out_late(t):
                if t >= 2:
                    pe.wait_ge(out_added, BEFORE_LATE + t - 1)
                else:
                    pe.wait_ge(qk_copied, 4 * LAST + 3 + t)
                out_tile(LAST - 2, t, proj[t % 2])

            def step(h, j):
                if is_last(h):
                    turn_probs(h)
                    project_out_late(B - 2)
                    attend(h, j, 0)
                    attend(h, j, 1)
                    project_out_late(B - 1)
                    return
                project_qk(h + 1, j)
                if is_first(h):
                    turn_probs(h)
                for half in range(2):
                    make_scores(h + 1, half)
                    attend(h, j, half)
                if j == GH - 1:
                    pe.wait_ge(lo_made, split_before(h) + 2)
                    for t in range(B):
                        if t < 2:
                            pe.wait_ge(qk_copied, 4 * (h + 1) + 3 + t)
                        else:
                            pe.wait_ge(v_copied, 2 * (h + 1) + t - 1)
                        project_v(t)
                if isinstance(h, int) and h == LAST - 1:
                    for t in range(B - 2):
                        project_out_late(t)
                elif j % 2 == 1 and not (isinstance(h, int) and h == LAST - 2):
                    project_out(h, j)

            pe.wait_ge(lo_made, split_k(0))
            for half in range(2):
                turn_x(HALF + 2 * half)
                turn_x(HALF + 2 * half + 1)
                pe.wait_ge(v_copied, B - 1 + half)
                project_half(0, 0, 0, half)
            pe.wait_ge(lo_made, split_k(0) + 1)
            for half in range(2):
                pe.wait_ge(qk_copied, half + 1)
                pe.wait_ge(x_lo_made, HALF * (half + 1))
                project_half(0, 0, 1, half)
            make_scores(0, 0)
            make_scores(0, 1)
            run_steps(pe, step)

            def last_out(t):
                if t >= 2:
                    pe.wait_ge(x1_made, t - 1)
                else:
                    pe.wait_ge(scores_biased, 2 * LAST + t + 1)
                out_tile(LAST, t, score[t % 2])

            def turn_y(t):
                pe.wait_ge(y_made, t + 1)
                if t >= 2:
                    pe.wait_ge(y_lo_made, t - 1)
                else:
                    pe.wait_ge(attn_lo_made, 2 * LAST + t + 1)
                for c in range(C):
                    ins = pe.transpose(attended[t % 2][:, c * P:(c + 1) * P], y_norm[t][:, c * P:(c + 1) * P],
                                       ident[:, :])
                ins.then_inc(y_turned, 1)

            def turned_y(t):
                at = slice(t * P, (t + 1) * P)
                return chunks(xT_hi[:, :, at], xT_lo[:, :, at])

            def project_ag(t):
                pe.wait_ge(y_copied, t + 1)
                if 2 <= t < B - 1:
                    pe.wait_ge(hw_lo_made, t - 1)
                elif t < 2:
                    pe.wait_ge(probsT_copied, 2 + t + 1)
                for c in range(C):
                    ins = pe.matmul(ag_bank(t)[:, 0:AG], y_whole[t % 2][:, c * P:(c + 1) * P], ag[:, c, :],
                                    start=(c == 0), stop=(c == C - 1))
                ins.then_inc(ag_projected, 1)

            def project_base(t):
                pe.wait_ge(y_lo_made, t + 1)
                if 2 <= t < B - 1:
                    pe.wait_ge(out_made, t - 1)
                elif t < 2:
                    pe.wait_ge(out_added, BEFORE_LATE + B - 1 + t)
                product(base_bank(t)[:, :], turned_y(t), chunks(wv_hi, wv_lo), stop=False)

            def turn_hw(t):
                pe.wait_ge(hw_made, t + 1)
                pe.transpose(ag_bank(t)[:, 2 * P:3 * P], hw[:, t % 2, :], ident[:, :]).then_inc(hw_turned, 1)

            def add_delta(t):
                pe.wait_ge(hw_lo_made, t + 1)
                product(base_bank(t)[:, :], [(hwT_hi[:, t % 2, :], hwT_lo[:, t % 2, :])], [(wb_hi, wb_lo)],
                        start=False).then_inc(delta_added, 1)

            pe.wait_ge(lo_made, split_before(H))
            pe.wait_ge(ag_loaded, 16)
            for t in range(4):
                last_out(t)
            turn_y(0)
            for t in range(B + 1):
                if t + 4 < B:
                    last_out(t + 4)
                if t + 1 < B:
                    turn_y(t + 1)
                if t < B - 1:
                    project_ag(t)
                if 1 <= t < B:
                    turn_hw(t - 1)
                if t == B - 2:
                    project_ag(B - 1)
                if t < B:
                    project_base(t)
                if t == B - 1:
                    turn_hw(B - 1)
                if t >= 1:
                    add_delta(t - 1)


def kernel(x, ctx_4096, mask_BxSxS2_bk0, g_xattn, g_ffn, L0_xattn_position_bias, L0_xattn_ln_weight, L0_xattn_w_q,
           L0_xattn_w_k, L0_xattn_w_v, L0_xattn_w_out, L0_ffn_W_base, L0_ffn_b_base, L0_ffn_W_gate, L0_ffn_A,
           L0_ffn_B):
    import numpy as np
    import concourse.bacc as bacc
    from concourse.bass_utils import run_bass_kernel_spmd

    def by_head(w):
        return np.asarray(w).reshape(H, P, C, P).transpose(0, 3, 2, 1).reshape(H, P, D)

    ag = np.concatenate([np.asarray(L0_ffn_A).reshape(ER, D), np.asarray(L0_ffn_W_gate)], axis=0)
    laid = {
        "x": x,
        "ctx": np.asarray(ctx_4096).reshape(B, P, C, P).transpose(3, 0, 2, 1).reshape(P, B, D),
        "mask": np.asarray(mask_BxSxS2_bk0).transpose(1, 0, 2),
        "gates": np.concatenate([np.asarray(g_xattn), np.asarray(g_ffn)]),
        "bias": L0_xattn_position_bias,
        "ln_w": np.asarray(L0_xattn_ln_weight).reshape(C, P).T,
        "w_q": by_head(L0_xattn_w_q),
        "w_k": by_head(L0_xattn_w_k),
        "w_v": np.asarray(L0_xattn_w_v).reshape(G, GH * P, C, P).transpose(0, 2, 3, 1).reshape(G * C, P, GH * P),
        "w_o": np.asarray(L0_xattn_w_out).T.reshape(H, P, D),
        "w_base": np.asarray(L0_ffn_W_base).T.reshape(C, P, D),
        "b_base": L0_ffn_b_base,
        "w_ag": ag.reshape(AG, C, P).transpose(2, 1, 0).reshape(P, C * AG),
        "w_b": np.asarray(L0_ffn_B).transpose(0, 2, 1).reshape(ER, D),
    }
    nc = bacc.Bacc("TRN2", target_bir_lowering=False, num_devices=1)
    arrays, args = {}, []
    for name, a in laid.items():
        a = np.ascontiguousarray(a)
        arrays[f"in_{name}"] = a
        args.append(nc.dram_tensor(f"in_{name}", a.shape, mybir.dt.from_np(a.dtype), kind="ExternalInput").ap())
    args.append(nc.dram_tensor("out_dram", (B, P, D), F32, kind="ExternalOutput").ap())
    program(nc, *args)
    r = run_bass_kernel_spmd(nc, [arrays], core_ids=[0])
    return r.results[0]["out_dram"]
```
